# Optimizing a Trainium2 kernel written in Bass

```python
import numpy as np
import jax
import jax.numpy as jnp

def _softmax(x, axis=-1):
    return jax.nn.softmax(x, axis=axis)

def _gelu(x):
    return jax.nn.gelu(x, approximate=True)

def _silu(x):
    return jax.nn.silu(x)

def _sigmoid(x):
    return jax.nn.sigmoid(x)

def _layernorm(x, axis=-1, eps=1e-05):
    m = jnp.mean(x, axis=axis, keepdims=True)
    v = jnp.var(x, axis=axis, keepdims=True)
    return (x - m) / jnp.sqrt(v + eps)

def _scatter_add(tgt, idx, src, axis=0):
    return tgt.at[idx].add(src)

def _segment_sum(src, seg, n):
    return jax.ops.segment_sum(src, seg, n)
kernel_name = 'mk_gnn_resnorm_d1_gnn_r8_204d5b'

def setup_inputs(seed: int=0):
    np.random.seed(seed)
    _w = jnp.asarray

    def _rec_inputs():
        import jax
        import jax.numpy as jnp
        _gk = jax.random.key(seed)
        x = -0.0001006 + 1 * jax.random.normal(jax.random.fold_in(_gk, 1), (12500, 96), jnp.float32)
        _s = jax.random.randint(jax.random.fold_in(_gk, 2), (200000,), 0, 12500, jnp.int32)
        _d = jax.random.randint(jax.random.fold_in(_gk, 3), (200000,), 0, 12500, jnp.int32)
        _loop = jnp.arange(12500, dtype=jnp.int32)
        src = jnp.concatenate([_s, _d, _loop])
        dst = jnp.concatenate([_d, _s, _loop])
        _o = jnp.argsort(dst, stable=True)
        src = src[_o]
        dst = dst[_o]
        edge_attr_4 = 0.000714719 + 1.00021 * jax.random.normal(jax.random.fold_in(_gk, 11), (412500, 4), jnp.float32)
        return (x, src, dst, edge_attr_4)
    x, src, dst, edge_attr_4 = _rec_inputs()

    def _L0_gnn_setup():
        import jax, jax.numpy as jnp
        import numpy as np
        EPS = 1e-05

        def _mlp(h, W, b, gamma, beta):
            h = jax.nn.relu(h @ W + b)
            mu = jnp.mean(h, axis=0)
            var = jnp.mean(jnp.square(h - mu), axis=0)
            return gamma * (h - mu) * jax.lax.rsqrt(var + EPS) + beta
        key = jax.random.key(seed)
        ks = jax.random.split(key, 10)
        N, E, C_in, C_out, E_dim = (6250, 100000, 96, 96, 4)
        x = jax.random.normal(ks[0], (N, C_in), dtype=jnp.float32)
        edge_index = jax.random.randint(ks[1], (2, E), 0, N, dtype=jnp.int64)
        edge_attr = jax.random.normal(ks[2], (E, E_dim), dtype=jnp.float32)
        s = lambda fan_in: 1.0 / np.sqrt(fan_in)
        W_node = jax.random.uniform(ks[3], (C_in, C_out), jnp.float32, -s(C_in), s(C_in))
        b_node = jnp.zeros((C_out,), jnp.float32)
        g_node = jnp.ones((C_out,), jnp.float32)
        beta_node = jnp.zeros((C_out,), jnp.float32)
        W_edge = jax.random.uniform(ks[4], (E_dim, C_out), jnp.float32, -s(E_dim), s(E_dim))
        b_edge = jnp.zeros((C_out,), jnp.float32)
        g_edge = jnp.ones((C_out,), jnp.float32)
        beta_edge = jnp.zeros((C_out,), jnp.float32)
        M_in = 2 * C_in + C_out
        W_msg = jax.random.uniform(ks[5], (M_in, C_out), jnp.float32, -s(M_in), s(M_in))
        b_msg = jnp.zeros((C_out,), jnp.float32)
        g_msg = jnp.ones((C_out,), jnp.float32)
        beta_msg = jnp.zeros((C_out,), jnp.float32)
        return dict(x=x, edge_index=edge_index, edge_attr=edge_attr, W_node=W_node, b_node=b_node, g_node=g_node, beta_node=beta_node, W_edge=W_edge, b_edge=b_edge, g_edge=g_edge, beta_edge=beta_edge, W_msg=W_msg, b_msg=b_msg, g_msg=g_msg, beta_msg=beta_msg)
    _L0_gnn_all = _L0_gnn_setup()
    _L0_gnn_in = {k: v for k, v in _L0_gnn_all.items() if k in ('W_node', 'b_node', 'g_node', 'beta_node', 'W_edge', 'b_edge', 'g_edge', 'beta_edge', 'W_msg', 'b_msg', 'g_msg', 'beta_msg')}
    del _L0_gnn_all
    return {'x': x, 'src': src, 'dst': dst, 'edge_attr_4': edge_attr_4, 'L0_gnn_W_node': _L0_gnn_in['W_node'], 'L0_gnn_b_node': _L0_gnn_in['b_node'], 'L0_gnn_g_node': _L0_gnn_in['g_node'], 'L0_gnn_beta_node': _L0_gnn_in['beta_node'], 'L0_gnn_W_edge': _L0_gnn_in['W_edge'], 'L0_gnn_b_edge': _L0_gnn_in['b_edge'], 'L0_gnn_g_edge': _L0_gnn_in['g_edge'], 'L0_gnn_beta_edge': _L0_gnn_in['beta_edge'], 'L0_gnn_W_msg': _L0_gnn_in['W_msg'], 'L0_gnn_b_msg': _L0_gnn_in['b_msg'], 'L0_gnn_g_msg': _L0_gnn_in['g_msg'], 'L0_gnn_beta_msg': _L0_gnn_in['beta_msg']}

def reference(x, src, dst, edge_attr_4, L0_gnn_W_node, L0_gnn_b_node, L0_gnn_g_node, L0_gnn_beta_node, L0_gnn_W_edge, L0_gnn_b_edge, L0_gnn_g_edge, L0_gnn_beta_edge, L0_gnn_W_msg, L0_gnn_b_msg, L0_gnn_g_msg, L0_gnn_beta_msg):
    import jax
    import jax.numpy as jnp

    def _L0_gnn_ref(x, edge_index, edge_attr, W_node, b_node, g_node, beta_node, W_edge, b_edge, g_edge, beta_edge, W_msg, b_msg, g_msg, beta_msg):
        import jax, jax.numpy as jnp
        import numpy as np
        EPS = 1e-05

        def _mlp(h, W, b, gamma, beta):
            h = jax.nn.relu(h @ W + b)
            mu = jnp.mean(h, axis=0)
            var = jnp.mean(jnp.square(h - mu), axis=0)
            return gamma * (h - mu) * jax.lax.rsqrt(var + EPS) + beta
        node_feat = _mlp(x, W_node, b_node, g_node, beta_node)
        edge_feat = _mlp(edge_attr, W_edge, b_edge, g_edge, beta_edge)
        row, col = (edge_index[0], edge_index[1])
        message = jnp.concatenate([x[row], x[col], edge_feat], axis=1)
        message = _mlp(message, W_msg, b_msg, g_msg, beta_msg)
        agg = jax.ops.segment_sum(message, col, num_segments=node_feat.shape[0])
        return agg + node_feat
    edge_index = jnp.stack([src, dst])
    x = _layernorm(x + _L0_gnn_ref(x, edge_index, edge_attr_4, L0_gnn_W_node, L0_gnn_b_node, L0_gnn_g_node, L0_gnn_beta_node, L0_gnn_W_edge, L0_gnn_b_edge, L0_gnn_g_edge, L0_gnn_beta_edge, L0_gnn_W_msg, L0_gnn_b_msg, L0_gnn_g_msg, L0_gnn_beta_msg), axis=-1)
    return x

_drawn_inputs = setup_inputs


def setup_inputs(seed=0):
    import zlib

    import numpy as np

    out = dict(_drawn_inputs(seed))
    spreads = {'L0_gnn_b_node': (0.0, 0.8),
     'L0_gnn_g_node': (1.0, 0.6),
     'L0_gnn_beta_node': (0.0, 0.8),
     'L0_gnn_b_edge': (0.0, 0.1),
     'L0_gnn_g_edge': (1.0, 0.2),
     'L0_gnn_beta_edge': (0.0, 0.388),
     'L0_gnn_b_msg': (0.0, 0.1),
     'L0_gnn_g_msg': (1.0, 0.2),
     'L0_gnn_beta_msg': (0.0, 0.1)}
    factors = {}
    for name, (base, spread) in spreads.items():
        noise = np.random.default_rng([zlib.crc32(name.encode()), seed]).standard_normal(out[name].shape)
        drawn = base * np.exp(spread * noise) if base else spread * noise
        out[name] = jnp.asarray(drawn.astype(out[name].dtype))
    for name, factor in factors.items():
        out[name] = (out[name] * factor).astype(out[name].dtype)
    return out
```

```python
from contextlib import ExitStack

import concourse.bass as bass
from concourse import mybir

F32 = mybir.dt.float32
BF16 = mybir.dt.bfloat16
I32 = mybir.dt.int32
ALU = mybir.AluOpType
ACT = mybir.ActivationFunctionType
AX = mybir.AxisListType

P = 128
TS = 8
SE = TS * P
PC = 2 * SE
W = 64
KB = 96
KZ = 96
RS = 24
NQ = 256
EPS = 1e-5
SINK = -1.0e30


def sizes(N, E):
    NS = -(-E // SE)
    while NS % 4 != 3:
        NS += 1
    NB = -(-(N + KB) // P)
    return NS, NB + -NB % 4


def gnn_kernel(nc, x, xT, srcT, dstT, dst_rows, eaT, W_node, b_node, g_node, beta_node, W_edge, b_edge,
               g_edge, beta_edge, W_msg, b_msg, g_msg, beta_msg, out, E):
    N, C = out.shape
    C1 = C + 1
    NS, NB = sizes(N, E)
    NT = NS * TS
    NP = NB * P
    ED, EP = eaT.shape
    NPC = EP // PC
    XP = 8
    XC = ED * EP // P // XP
    SPLIT = XC + 3 * (XC // 2)
    NQS = NP // NQ
    HX = C1 + W
    assert C == 96 and ED == 4 and EP == (NS + 1) * SE and NPC % 2 == 0 and NS > RS

    tabA = nc.dram_tensor("tabA", (NP + 1, C), F32).ap()
    tabB = nc.dram_tensor("tabB", (NP, C), F32).ap()
    nodeT = nc.dram_tensor("nodeT", (C, NP), F32).ap()
    stack = nc.dram_tensor("stack", (32, EP), BF16).ap()
    dloc_rows = nc.dram_tensor("dloc_rows", (NS, SE), BF16).ap()
    ea_flat = eaT.rearrange("r (k c) -> (r k) c", k=P // ED)
    stack_flat = [stack[4 * g:4 * g + 4, :].rearrange("r (k c) -> (r k) c", k=P // ED) for g in range(6)]

    with ExitStack() as ctx:
        def sb(name, shape, dt=F32):
            return ctx.enter_context(nc.sbuf_tensor(name, shape, dt))

        def sem(name):
            return ctx.enter_context(nc.semaphore(name))

        room = sb("room", [P, max(NP, 2 * SPLIT + EP // P // 2)])
        S = room[0:C1, 0:NP]
        G = sb("G", [P, RS, TS * C])
        rE = sb("rE", [C1, 2, SE])
        OHT = sb("OHT", [KB, 2, SE])
        HXb = sb("HXb", [P, 2, TS, HX])
        Hpre = sb("Hpre", [P, 2, TS * C])
        eaS = sb("eaS", [KZ, 2, PC], BF16)
        dlB = sb("dlB", [KB, 2, SE], BF16)
        Bw = sb("Bw", [KB, 2, C])
        dloc = sb("dloc", [P, NT], BF16)
        idx_all = sb("idx_all", [P, srcT.shape[1]], I32)
        idx = sb("idx", [P, RS * TS], I32)
        base = sb("base", [1, NS], I32)
        basef = sb("basef", [1, NS])
        ident = sb("ident", [P, P])
        ones = sb("ones", [P, P])
        iota_w = sb("iota_w", [P, W], BF16)
        iota_p = sb("iota_p", [P, 1])
        w12 = sb("w12", [C1, 2 * C])
        w3 = sb("w3", [C, C])
        w3p = sb("w3p", [C1, C])
        wn = sb("wn", [C1, C])
        we = sb("we", [5, 3, C])
        we16 = sb("we16", [5, 3, C], BF16)
        weS = sb("weS", [KZ, C], BF16)
        vec = sb("vec", [C, 4])
        rows = sb("rows", [C1, 2, C])
        col = sb("col", [C, 16])
        rw = sb("rw", [C1, 9, C])
        sumR = sb("sumR", [C, NPC])
        sumQ = sb("sumQ", [C, NPC])
        nsR = sb("nsR", [C, NQS])
        nsQ = sb("nsQ", [C, NQS])
        gacc = sb("gacc", [C1, C])
        gI = sb("gI", [C, C])
        Mm = sb("Mm", [C1, C])
        Mn = sb("Mn", [C1, C])
        flag = sb("flag", [P, 4])
        flagi = sb("flagi", [1, 1], I32)
        sink = sb("sink", [1, C])
        zero8 = sb("zero8", [8, EP - E], BF16)
        bst = sb("bst", [P, 2, 4, 6])
        mv = sb("mv", [P, 2, 4, 2])
        sd = sb("sd", [P, 2, 2, 4])
        epsc = sb("epsc", [P, 1])
        ps = ctx.enter_context(nc.psum_tensor("ps", [P, 8, 512], F32))

        xres = G[:, 0:2, 0:4 * C]
        y = G[:, 2:4, 0:4 * C]
        yo = G[:, 4:6, 0:4 * C]

        HXf = HXb[:, :, :, :].rearrange("p b t n -> p (b t n)")
        xc = HXf[0:C1, 0:2 * NQ].rearrange("c (b n) -> c b n", b=2)
        nR = HXf[0:C, 2 * NQ:4 * NQ].rearrange("c (b n) -> c b n", b=2)
        abS = HXf[:, 4 * NQ:4 * NQ + 8 * C].rearrange("p (b n) -> p b n", b=2)
        Sc = HXb[0:C1, :, :, :].rearrange("c b t n -> c b (t n)")[:, :, 0:512]

        g_rowA, g_rowB, iota_g, oh_g = G[:, 0, 0:C], G[:, 1, 0:C], G[:, 2, 0:512], G[:, 3, 0:512]
        dst_g, NG = flag[:, 0:1], NP // 512

        part = [room[:, b * SPLIT:b * SPLIT + XC] for b in range(2)]
        piece = [[room[:, b * SPLIT + XC + g * XC // 2:b * SPLIT + XC + (g + 1) * XC // 2].bitcast(BF16)
                  for g in range(3)] for b in range(2)]
        ones16 = room[:, 2 * SPLIT:2 * SPLIT + EP // P // 2].bitcast(BF16)
        Gi = G[:, :, :].rearrange("p a b -> p (a b)")
        dst_t = Gi[:, 0:NT].bitcast(I32)
        NDR = -(-NS // P)
        dst_r = [Gi[:, NT + k * SE:NT + (k + 1) * SE].bitcast(I32) for k in range(NDR)]
        loc_r = [Gi[:, NT + NDR * SE + k * SE // 2:NT + NDR * SE + (k + 1) * SE // 2].bitcast(BF16)
                 for k in range(NDR)]
        assert NT + NDR * SE * 3 // 2 <= RS * TS * C and NS <= 512
        Rst = [rE[0:C, :, :].rearrange("c b n -> c (b n)"), OHT[0:C, :, :].rearrange("c b n -> c (b n)")]

        w_in = sem("w_in")
        dst_in = sem("dst_in")
        idx_in = sem("idx_in")
        we_in = sem("we_in")
        xc_in = [sem(f"xc_in{b}") for b in range(2)]
        ab_out = [sem(f"ab_out{b}") for b in range(2)]
        nR_out = [sem(f"nR_out{b}") for b in range(2)]
        sink_out = sem("sink_out")
        part_in = [sem(f"part_in{b}") for b in range(2)]
        piece_out = [sem(f"piece_out{b}") for b in range(2)]
        ones_out = sem("ones_out")
        zero_out = sem("zero_out")
        loc_out = sem("loc_out")
        ea_in = [sem(f"ea_in{b}") for b in range(2)]
        dl_in = [sem(f"dl_in{b}") for b in range(2)]
        bw_in = [sem(f"bw_in{b}") for b in range(2)]
        gathered = [sem(f"gathered{b}") for b in range(2)]
        fin_in = [sem(f"fin_in{b}") for b in range(2)]
        y_out = [sem(f"y_out{b}") for b in range(2)]
        consts = sem("consts")
        small_set = sem("small_set")
        zeros_set = sem("zeros_set")
        ea_zero_set = sem("ea_zero_set")
        ones_set = sem("ones_set")
        chain = sem("chain")
        ident_zero = sem("ident_zero")
        we_split = sem("we_split")
        basef_done = sem("basef_done")
        baseb_done = sem("baseb_done")
        dloc_done = sem("dloc_done")
        loc_done = sem("loc_done")
        badp_done = sem("badp_done")
        bad_done = sem("bad_done")
        flag_done = sem("flag_done")
        ab_pe = sem("ab_pe")
        ab_act = sem("ab_act")
        nsq_done = sem("nsq_done")
        split_done = sem("split_done")
        st_pe = sem("st_pe")
        st_relu = sem("st_relu")
        st_sq = sem("st_sq")
        var_done = sem("var_done")
        sd_done = sem("sd_done")
        shift_done = sem("shift_done")
        const_done = sem("const_done")
        w3p_done = sem("w3p_done")
        Mn_row_done = sem("Mn_row_done")
        idx_done = sem("idx_done")
        pool_turn = sem("pool_turn")
        dve_turn = sem("dve_turn")
        z_done = sem("z_done")
        relz_done = sem("relz_done")
        oht_done = sem("oht_done")
        oh_done = sem("oh_done")
        hmm_done = sem("hmm_done")
        hpre_done = sem("hpre_done")
        hx_done = sem("hx_done")
        scat_done = sem("scat_done")
        sadd_done = sem("sadd_done")
        gen_set = sem("gen_set")
        gen_free = sem("gen_free")
        gen_in = sem("gen_in")
        gen_idx = sem("gen_idx")
        gen_rows = sem("gen_rows")
        gen_z = sem("gen_z")
        gen_relz = sem("gen_relz")
        gen_mm = sem("gen_mm")
        gen_dst = sem("gen_dst")
        gen_half = sem("gen_half")
        gen_pre = sem("gen_pre")
        gen_h = sem("gen_h")
        gen_gram = sem("gen_gram")
        gen_gacc = sem("gen_gacc")
        gen_oh = sem("gen_oh")
        gen_sum = sem("gen_sum")
        gen_add = sem("gen_add")
        gI_done = sem("gI_done")
        msum_done = sem("msum_done")
        mvar_done = sem("mvar_done")
        msd_done = sem("msd_done")
        mscale_done = sem("mscale_done")
        mb_done = sem("mb_done")
        M_done = sem("M_done")
        Sc_done = sem("Sc_done")
        f_pe = sem("f_pe")
        f_y = sem("f_y")
        f_bn = sem("f_bn")
        f_mv = sem("f_mv")
        f_sd = sem("f_sd")
        f_rs = sem("f_rs")
        f_out = sem("f_out")

        NW = 15
        HALF = RS // 2
        RINGS = NS // RS
        QF = N // 512
        REST = N - 512 * QF
        assert QF % 2 == 0 and REST and NP == 512 * (QF + 1)

        block = ctx.enter_context(nc.Block())

        @block.sync
        def _(sp):
            for dst, src in ((w12[0:C, 0:C], W_msg[0:C, :]), (w12[0:C, C:2 * C], W_msg[C:2 * C, :]),
                             (w12[C:C1, C:2 * C], b_msg[None, :]), (wn[0:C, :], W_node),
                             (wn[C:C1, :], b_node[None, :]), (w3[:, :], W_msg[2 * C:3 * C, :]),
                             (we[0:4, 0, :], W_edge), (we[4:5, 0, :], b_edge[None, :]),
                             (rows[C:C1, 0, :], g_msg[None, :]), (rows[C:C1, 1, :], beta_msg[None, :])):
                sp.dma_start(dst, src).then_inc(w_in, 16)
            with nc.allow_non_contiguous_dma(reason="four vectors as columns, and each super's first dst"):
                for k, v in enumerate((g_edge, beta_edge, g_node, beta_node)):
                    sp.dma_start(vec[:, k:k + 1], v[:, None]).then_inc(w_in, 16)
                sp.dma_start(base[0:1, :], dst_rows[:, 0:1].rearrange("s o -> o s")).then_inc(w_in, 16)
            sp.dma_start(dst_t, dstT).then_inc(dst_in, 16)
            for k in range(NDR):
                n = min(P, NS - k * P)
                sp.dma_start(dst_r[k][0:n, :], dst_rows[k * P:k * P + n, :]).then_inc(dst_in, 16)
            for b in range(2):
                sp.dma_start(part[b], ea_flat[:, b * XC:(b + 1) * XC]).then_inc(part_in[b], 16)
            sp.dma_start(idx_all[:, :], srcT).then_inc(idx_in, 16)
            sp.wait_ge(small_set, 3)
            sp.dma_start(tabA[NP:NP + 1, :], sink[:, :]).then_inc(sink_out, 16)
            sp.wait_ge(we_split, 3)
            sp.wait_ge(zeros_set, 3)
            for r, g in enumerate((0, 1, 2, 0, 1, 0)):
                sp.dma_start(weS[4 * r:4 * r + 4, :], we16[0:4, g, :]).then_inc(we_in, 16)
            for g in range(3):
                sp.dma_start(weS[24 + g:25 + g, :], we16[4:5, g, :]).then_inc(we_in, 16)
            sp.wait_ge(loc_done, NDR)
            for k in range(NDR):
                n = min(P, NS - k * P)
                sp.dma_start(dloc_rows[k * P:k * P + n, :], loc_r[k][0:n, :]).then_inc(loc_out, 16)
            for r in range(8):
                sp.dma_start(stack[24 + r:25 + r, :].rearrange("o (p c) -> (o p) c", p=P), ones16)\
                    .then_inc(ones_out, 16)
            for k in range(XP):
                b = k % 2
                sp.wait_ge(split_done, k + 1)
                for r, g in enumerate((0, 0, 0, 1, 1, 2)):
                    sp.dma_start(stack_flat[r][:, k * XC:(k + 1) * XC], piece[b][g]).then_inc(piece_out[b], 16)
                if k + 2 < XP:
                    sp.wait_ge(piece_out[b], 96 * (k // 2 + 1))
                    sp.dma_start(part[b], ea_flat[:, (k + 2) * XC:(k + 3) * XC]).then_inc(part_in[b], 16)
            sp.wait_ge(ones_out, 128)
            sp.dma_start(stack[24:32, E:EP], zero8[:, :]).then_inc(zero_out, 16)

            for b in range(2):
                sp.wait_ge(piece_out[b], 96 * XP // 2)
            sp.wait_ge(zero_out, 16)
            sp.wait_ge(ea_zero_set, 1)
            for c in range(2):
                sp.dma_start(eaS[0:32, c, :], stack[:, c * PC:(c + 1) * PC]).then_inc(ea_in[c], 16)
            with sp.Fori(0, NPC // 2 - 1) as i:
                for b in range(2):
                    sp.wait_ge(st_pe, 2 * i + b + 1)
                    sp.dma_start(eaS[0:32, b, :], stack[:, bass.ds((2 * i + b + 2) * PC, PC)])\
                        .then_inc(ea_in[b], 16)

            def load_ea(s, b):
                sp.dma_start(eaS[0:32, b, 0:SE], stack[:, bass.ds(s * SE, SE)]).then_inc(ea_in[b], 16)

            def load_dl(s, b):
                sp.dma_start(dlB[:, b, :], dloc_rows[bass.ds(s, 1), :].to_broadcast([KB, SE]))\
                    .then_inc(dl_in[b], 16)

            def load_bw(s, b):
                first = sp.value_load(base[0:1, bass.ds(s, 1)], min_val=0, max_val=N)
                sp.dma_start(Bw[:, b, :], tabB[bass.ds(first, KB), :]).then_inc(bw_in[b], 16)

            sp.wait_ge(st_pe, NPC)
            sp.wait_ge(st_sq, NPC)
            sp.wait_ge(loc_out, 16 * NDR)
            for b in range(2):
                sp.wait_ge(ab_out[b], 16 * NQS)
            for s in range(2):
                load_ea(s, s)
                load_dl(s, s)
                load_bw(s, s)
            with sp.Fori(0, (NS - 3) // 2) as i:
                for b in range(2):
                    s = 2 * i + b + 2
                    sp.wait_ge(z_done, s - 1)
                    load_ea(s, b)
                    sp.wait_ge(oht_done, s - 1)
                    load_dl(s, b)
                    sp.wait_ge(hmm_done, s - 1)
                    load_bw(s, b)
            sp.wait_ge(z_done, NS - 2)
            load_ea(NS - 1, 0)
            sp.wait_ge(oht_done, NS - 2)
            load_dl(NS - 1, 0)
            sp.wait_ge(hmm_done, NS - 2)
            load_bw(NS - 1, 0)

            sp.wait_ge(flag_done, 1)
            with sp.If(sp.value_load(flagi[0:1, 0:1], min_val=0, max_val=2 * P) > 0):
                with sp.Fori(0, NT) as t:
                    sp.wait_ge(gen_free, t + 1)
                    sp.dma_start(eaS[0:32, 0, 0:P], stack[:, bass.ds(t * P, P)]).then_inc(gen_in, 16)
                    with nc.allow_non_contiguous_dma(reason="128 values of dst"):
                        sp.dma_start(idx[:, 1:2], dstT[:, bass.ds(t, 1)]).then_inc(gen_in, 16)
                sp.wait_ge(gen_free, NT + 1)

            def load_fin(q, b):
                sp.dma_start(rE[0:C, b, 0:512], nodeT[:, bass.ds(q * 512, 512)]).then_inc(fin_in[b], 16)
                sp.dma_start(xres[:, b, :].rearrange("p (k c) -> p k c", k=4),
                             x[bass.ds(q * 512, 512), :].rearrange("(k p) c -> p k c", p=P)).then_inc(fin_in[b], 16)

            def store_fin(q, b):
                sp.wait_ge(f_out, 4 * q + 4)
                sp.dma_start(out[bass.ds(q * 512, 512), :].rearrange("(k p) c -> p k c", p=P),
                             yo[:, b, :].rearrange("p (k c) -> p k c", k=4)).then_inc(y_out[b], 16)

            sp.wait_ge(hpre_done, NS)
            sp.wait_ge(hmm_done, NS)
            for b in range(2):
                sp.wait_ge(nR_out[b], 8 * NQS)
            for b in range(2):
                load_fin(b, b)
            with sp.Fori(0, QF // 2 - 1) as i:
                for b in range(2):
                    q = 2 * i + b
                    store_fin(q, b)
                    sp.wait_ge(f_pe, q + 1)
                    load_fin(q + 2, b)
            store_fin(QF - 2, 0)
            load_fin(QF, 0)
            store_fin(QF - 1, 1)
            sp.wait_ge(f_out, 4 * QF + 4)
            for k in range(-(-REST // P)):
                n = min(P, REST - k * P)
                sp.dma_start(out[QF * 512 + k * P:QF * 512 + k * P + n, :], yo[0:n, 0, k * C:(k + 1) * C])\
                    .then_inc(y_out[0], 16)
            sp.wait_ge(y_out[0], 16 * (QF // 2 - (-REST // P)))
            sp.wait_ge(y_out[1], 16 * (QF // 2))

        @block.gpsimd
        def _(pool):
            pool.memset(ones[:, :], 1.0).then_inc(consts, 1)
            pool.memset(ident[:, :], 0.0).then_inc(ident_zero, 1)
            pool.iota(iota_w[:, :], [[1, W]], base=0, channel_multiplier=0,
                      allow_small_or_imprecise_dtypes=True).then_inc(consts, 1)
            pool.iota(iota_p[:, :], [[0, 1]], base=0, channel_multiplier=1,
                      allow_small_or_imprecise_dtypes=True).then_inc(consts, 1)
            pool.wait_ge(ident_zero, 1)
            pool.affine_select(out=ident[:, :], in_=ident[:, :], compare_op=ALU.not_equal, fill=1.0, base=0,
                               pattern=[[-1, P]], channel_multiplier=1).then_inc(consts, 1)

            def copy_idx(col, half):
                pool.tensor_copy(idx[:, half * HALF * TS:(half + 1) * HALF * TS],
                                 idx_all[:, bass.ds(col, HALF * TS)]).then_inc(idx_done, 1)

            def gather(j):
                for t in range(TS):
                    pool.indirect_dma_start(G[:, j, t * C:(t + 1) * C], None, tabA,
                                            bass.IndirectOffsetOnAxis(ap=idx[:, j * TS + t:j * TS + t + 1], axis=0))\
                        .then_inc(gathered[j % 2], 16)

            pool.wait_ge(idx_in, 16)
            copy_idx(0, 0)
            copy_idx(HALF * TS, 1)
            for b in range(2):
                pool.wait_ge(ab_out[b], 16 * NQS)
            pool.wait_ge(sink_out, 16)
            pool.wait_ge(dloc_done, 1)
            pool.wait_ge(loc_out, 16 * NDR)
            pool.wait_ge(idx_done, 2)
            for j in range(RS):
                if j >= 2:
                    pool.wait_ge(gathered[j % 2], 16 * TS * (j // 2))
                gather(j)
                if j == HALF + 2:
                    copy_idx(RS * TS, 0)
            if RINGS > 1:
                with pool.Fori(1, RINGS) as it:
                    for j in range(RS):
                        s = it * RS + j
                        if j == 0:
                            pool.wait_ge(idx_done, 2 * it + 1)
                        if j == HALF:
                            pool.wait_ge(idx_done, 2 * it + 2)
                        pool.wait_ge(gathered[j % 2], (it * (RS // 2) + j // 2) * (16 * TS))
                        pool.wait_ge(hpre_done, s - RS + 1)
                        pool.sem_inc(pool_turn, 1)
                        gather(j)
                        if j == 2:
                            copy_idx(it * (RS * TS) + HALF * TS, 1)
                        if j == HALF + 2:
                            copy_idx((it + 1) * (RS * TS), 0)
            for s in range(RINGS * RS, NS):
                j = s - RINGS * RS
                if j == 0:
                    pool.wait_ge(idx_done, 2 * RINGS + 1)
                if j == HALF:
                    pool.wait_ge(idx_done, 2 * RINGS + 2)
                pool.wait_ge(gathered[j % 2], 16 * TS * (s // 2))
                pool.wait_ge(hpre_done, s - RS + 1)
                gather(j)
                if j == 2:
                    copy_idx(RINGS * RS * TS + HALF * TS, 1)

            pool.wait_ge(sadd_done, 2 * NS)
            pool.wait_ge(flag_done, 1)
            with pool.If(pool.value_load(flagi[0:1, 0:1], min_val=0, max_val=2 * P) > 0):
                pool.iota(iota_g, [[1, 512]], base=0, channel_multiplier=0,
                          allow_small_or_imprecise_dtypes=True).then_inc(gen_set, 1)
                with pool.Fori(0, NT) as t:
                    pool.wait_ge(gen_free, t + 1)
                    pool.sem_inc(pool_turn, 1)
                    pool.tensor_copy(idx[:, 0:1], idx_all[:, bass.ds(t, 1)]).then_inc(gen_idx, 1)
                    pool.wait_ge(gen_idx, t + 1)
                    pool.sem_inc(pool_turn, 1)
                    pool.wait_ge(gen_in, 32 * t + 32)
                    pool.sem_inc(pool_turn, 1)
                    pool.indirect_dma_start(g_rowA, None, tabA, bass.IndirectOffsetOnAxis(ap=idx[:, 0:1], axis=0))\
                        .then_inc(gen_rows, 16)
                    pool.indirect_dma_start(g_rowB, None, tabB, bass.IndirectOffsetOnAxis(ap=idx[:, 1:2], axis=0))\
                        .then_inc(gen_rows, 16)
                pool.wait_ge(gen_free, NT + 1)

            for b in range(2):
                pool.tensor_copy(Sc[:, b, :], S[:, b * 512:(b + 1) * 512]).then_inc(Sc_done, 1)
            with pool.Fori(0, QF // 2 - 1) as i:
                for b in range(2):
                    pool.wait_ge(f_pe, 2 * i + b + 1)
                    pool.sem_inc(pool_turn, 1)
                    pool.tensor_copy(Sc[:, b, :], S[:, bass.ds((2 * i + b + 2) * 512, 512)]).then_inc(Sc_done, 1)
            pool.wait_ge(f_pe, QF - 1)
            pool.tensor_copy(Sc[:, 0, :], S[:, QF * 512:(QF + 1) * 512]).then_inc(Sc_done, 1)

        @block.scalar
        def _(act):
            for b in range(2):
                act.dma_start(xc[:, b, :], xT[:, b * NQ:(b + 1) * NQ]).then_inc(xc_in[b], 16)

            def table_step(q, b, turn, last):
                act.wait_ge(ab_pe, q + 1)
                if turn is not None:
                    act.wait_ge(ab_out[b], turn * 32)
                act.activation(abS[:, b, :], ps[:, b, 0:4 * C], ACT.Copy).then_inc(ab_act, 1)
                if turn is not None:
                    act.wait_ge(nR_out[b], turn * 16)
                act.activation(nR[:, b, :], ps[0:C, 2 + b, 0:NQ], ACT.Relu, accum_out=nsR[:, bass.ds(q, 1)])\
                    .then_inc(ab_act, 1)
                if not last:
                    act.dma_start(xc[:, b, :], xT[:, bass.ds((q + 2) * NQ, NQ)]).then_inc(xc_in[b], 16)
                act.wait_ge(ab_act, 2 * q + 2)
                for k, tab in enumerate((tabA, tabB)):
                    act.dma_start(tab[bass.ds(q * NQ, NQ), :].rearrange("(h p) c -> p h c", p=P),
                                  abS[:, b, :].rearrange("p (h n) -> p h n", h=2)[:, :, k * C:(k + 1) * C])\
                        .then_inc(ab_out[b], 16)
                act.dma_start(nodeT[:, bass.ds(q * NQ, NQ)], nR[:, b, :]).then_inc(nR_out[b], 16)
                act.activation(ps[0:C, 4 + b, 0:NQ], nR[:, b, :], ACT.Square, accum_out=nsQ[:, bass.ds(q, 1)])\
                    .then_inc(nsq_done, 1)

            for b in range(2):
                table_step(b, b, None, False)
            with act.Fori(1, NQS // 2 - 1) as i:
                for b in range(2):
                    table_step(2 * i + b, b, i, False)
            for b in range(2):
                table_step(NQS - 2 + b, b, NQS // 2 - 1, True)

            def relu_step(c, b, waits):
                act.wait_ge(st_pe, c + 1)
                if waits:
                    act.wait_ge(st_sq, c - 1)
                act.activation(Rst[b], ps[0:C, 4 * b:4 * b + 4, :].rearrange("c b n -> c (b n)"), ACT.Relu,
                               accum_out=sumR[:, bass.ds(c, 1)]).then_inc(st_relu, 1)

            act.wait_ge(nsq_done, NQS)
            for b in range(2):
                relu_step(b, b, False)
            with act.Fori(1, NPC // 2) as i:
                for b in range(2):
                    relu_step(2 * i + b, b, True)
            act.wait_ge(small_set, 3)
            act.wait_ge(var_done, 1)
            act.activation(col[:, 8:10], col[:, 2:4], ACT.Sqrt, bias=epsc[0:C, :]).then_inc(sd_done, 1)

            def relz(s, b):
                act.wait_ge(z_done, s + 1)
                act.activation(rE[0:C, b, :], ps[0:C, 0:2, :].rearrange("c b n -> c (b n)"), ACT.Relu)\
                    .then_inc(relz_done, 1)

            def relh(s, b):
                act.wait_ge(hpre_done, s + 1)
                act.activation(HXb[:, b, :, 0:C], Hpre[:, b, :].rearrange("p (t c) -> p t c", t=TS), ACT.Relu)\
                    .then_inc(hx_done, 1)

            act.wait_ge(st_sq, NPC)
            relz(0, 0)
            relz(1, 1)
            relh(0, 0)
            act.wait_ge(hmm_done, 1)
            relz(2, 0)
            relh(1, 1)
            with act.Fori(1, (NS - 1) // 2) as i:
                for b in range(2):
                    s = 2 * i + b
                    act.wait_ge(hmm_done, s)
                    relz(s + 1, 1 - b)
                    act.wait_ge(scat_done, s - 1)
                    relh(s, b)
            act.wait_ge(scat_done, NS - 2)
            relh(NS - 1, 0)

            act.wait_ge(flag_done, 1)
            with act.If(act.value_load(flagi[0:1, 0:1], min_val=0, max_val=2 * P) > 0):
                with act.Fori(0, NT) as t:
                    act.wait_ge(gen_z, t + 1)
                    act.activation(rE[0:C, 0, 0:P], ps[0:C, 0, 0:P], ACT.Relu).then_inc(gen_relz, 1)
                    act.wait_ge(gen_pre, t + 1)
                    act.activation(HXb[:, 0, 0, 0:C], Hpre[:, 0, 0:C], ACT.Relu).then_inc(gen_h, 1)

            act.wait_ge(mvar_done, 1)
            act.activation(rw[C:C1, 5, :], rw[C:C1, 4, :], ACT.Sqrt, bias=epsc[C:C1, :]).then_inc(msd_done, 1)

            def fin_sd(q, b, first):
                act.wait_ge(f_mv, 4 * q + 4)
                if not first:
                    act.wait_ge(f_rs, q - 1)
                act.activation(sd[:, b, 0, :], mv[:, b, :, 1:2].rearrange("p k o -> p (k o)"), ACT.Sqrt,
                               bias=epsc[:, :]).then_inc(f_sd, 1)

            for b in range(2):
                fin_sd(b, b, True)
            with act.Fori(1, QF // 2) as i:
                for b in range(2):
                    fin_sd(2 * i + b, b, False)
            fin_sd(QF, 0, False)

        @block.tensor
        def _(pe):
            pe.wait_ge(consts, 4)
            pe.wait_ge(basef_done, 1)
            pe.matmul(ps[:, 7, 0:NS], ones[0:1, :], basef[0:1, :], start=True, stop=True).then_inc(baseb_done, 1)
            pe.wait_ge(w_in, 16 * NW)
            pe.wait_ge(small_set, 3)

            def table_step(q, b, turn, first=False):
                pe.wait_ge(xc_in[b], turn * 16 + 16)
                if not first:
                    pe.wait_ge(nsq_done, q - 1)
                for k in range(2):
                    pe.matmul(ps[:, b, k * 2 * C:(k + 1) * 2 * C], xc[:, b, k * P:(k + 1) * P], w12[:, :],
                              start=True, stop=True)
                pe.matmul(ps[0:C, 2 + b, 0:NQ], wn[:, :], xc[:, b, :], start=True, stop=True).then_inc(ab_pe, 1)

            for b in range(2):
                table_step(b, b, 0, True)
            with pe.Fori(1, NQS // 2) as i:
                for b in range(2):
                    table_step(2 * i + b, b, i)
            pe.wait_ge(badp_done, 2)
            pe.matmul(ps[0:1, 6, 0:2], ones[:, 0:1], flag[:, 2:4], start=True, stop=True).then_inc(bad_done, 1)

            def stat_step(c, b, turn, first=False):
                pe.wait_ge(ea_in[b], turn * 16 + 16)
                if not first:
                    pe.wait_ge(st_relu, c - 1)
                for k in range(PC // 512):
                    last = pe.matmul(ps[0:C, 4 * b + k, :], weS[:, :], eaS[:, b, 512 * k:512 * k + 512],
                                     start=True, stop=True)
                last.then_inc(st_pe, 1)

            pe.wait_ge(we_in, 16 * 9)
            pe.wait_ge(ea_zero_set, 1)
            pe.wait_ge(nsq_done, NQS)
            pe.wait_ge(ab_act, 2 * NQS)
            pe.wait_ge(dloc_done, 1)
            pe.wait_ge(flag_done, 1)
            for b in range(2):
                stat_step(b, b, 0, True)
            with pe.Fori(1, NPC // 2) as i:
                for b in range(2):
                    stat_step(2 * i + b, b, i)
            pe.wait_ge(st_relu, NPC)
            pe.wait_ge(shift_done, 1)
            pe.matmul(ps[C:C1, 2, 0:C], col[:, 12:13], w3[:, :], start=True, stop=True).then_inc(const_done, 1)
            pe.matmul(ps[C:C1, 3, 0:C], col[:, 13:14], ident[0:C, 0:C], start=True, stop=True)\
                .then_inc(const_done, 1)

            def zmm(s, b, n):
                pe.wait_ge(ea_in[b], n * 16)
                for k in range(2):
                    last = pe.matmul(ps[0:C, k, :], weS[:, :], eaS[:, b, 512 * k:512 * k + 512],
                                     start=True, stop=True)
                last.then_inc(z_done, 1)

            def hmm(s, b, n):
                pe.wait_ge(bw_in[b], n * 16)
                pe.wait_ge(oht_done, s + 1)
                for t in range(TS):
                    o = ps[:, 2 + 2 * b + t // 4, (t % 4) * C:(t % 4 + 1) * C]
                    pe.matmul(o, rE[:, b, t * P:(t + 1) * P], w3p[:, :], start=True, stop=False)
                    last = pe.matmul(o, OHT[:, b, t * P:(t + 1) * P], Bw[:, b, :], start=False, stop=True)
                last.then_inc(hmm_done, 1)

            def scat(s, b):
                pe.wait_ge(hx_done, s + 1)
                pe.wait_ge(oh_done, s + 1)
                for t in range(TS):
                    last = pe.matmul(ps[0:C1, 6 + b, 0:HX], HXb[:, b, t, 0:C1], HXb[:, b, t, :],
                                     start=(t == 0), stop=(t == TS - 1))
                last.then_inc(scat_done, 1)

            pe.wait_ge(w3p_done, 2)
            pe.wait_ge(Mn_row_done, 1)
            pe.wait_ge(ones_set, 2)
            zmm(0, 0, NPC // 2 + 1)
            pe.wait_ge(relz_done, 1)
            zmm(1, 1, NPC // 2 + 1)
            hmm(0, 0, 1)
            pe.wait_ge(relz_done, 2)
            zmm(2, 0, NPC // 2 + 2)
            hmm(1, 1, 1)
            scat(0, 0)
            pe.wait_ge(relz_done, 3)
            zmm(3, 1, NPC // 2 + 2)
            pe.wait_ge(hpre_done, 1)
            hmm(2, 0, 2)
            scat(1, 1)
            with pe.Fori(1, (NS - 1) // 2 - 1) as i:
                for u in range(2):
                    s = 2 * i + u + 1
                    b = (u + 1) % 2
                    pe.wait_ge(relz_done, s + 1)
                    zmm(s + 1, 1 - b, i + NPC // 2 + 2)
                    pe.wait_ge(hpre_done, s - 1)
                    hmm(s, b, i + (1 if u == 0 else 2))
                    pe.wait_ge(sadd_done, 2 * s - 4)
                    scat(s - 1, 1 - b)
            s = NS - 2
            pe.wait_ge(relz_done, s + 1)
            zmm(s + 1, 0, NPC // 2 + (NS + 1) // 2)
            pe.wait_ge(hpre_done, s - 1)
            hmm(s, 1, (NS - 1) // 2)
            pe.wait_ge(sadd_done, 2 * s - 4)
            scat(s - 1, 0)
            s = NS - 1
            pe.wait_ge(relz_done, s + 1)
            pe.wait_ge(hpre_done, s - 1)
            hmm(s, 0, (NS + 1) // 2)
            pe.wait_ge(sadd_done, 2 * s - 4)
            scat(s - 1, 1)
            pe.wait_ge(sadd_done, 2 * s - 2)
            scat(s, 0)

            pe.wait_ge(flag_done, 1)
            with pe.If(pe.value_load(flagi[0:1, 0:1], min_val=0, max_val=2 * P) > 0):
                with pe.Fori(0, NT) as t:
                    pe.wait_ge(gen_in, 32 * t + 32)
                    pe.matmul(ps[0:C, 0, 0:P], weS[:, :], eaS[:, 0, 0:P], start=True, stop=True).then_inc(gen_z, 1)
                    pe.wait_ge(gen_relz, t + 1)
                    pe.matmul(ps[:, 2, 0:C], rE[:, 0, 0:P], w3p[:, :], start=True, stop=True).then_inc(gen_mm, 1)
                    pe.wait_ge(gen_h, t + 1)
                    pe.matmul(ps[0:C1, 4, 0:C], HXb[:, 0, 0, 0:C1], HXb[:, 0, 0, 0:C],
                              start=True, stop=True).then_inc(gen_gram, 1)
                    with pe.Fori(0, NG) as k:
                        pe.wait_ge(gen_oh, t * NG + k + 1)
                        pe.matmul(ps[0:C1, 3, :], HXb[:, 0, 0, 0:C1], oh_g, start=True, stop=True)\
                            .then_inc(gen_sum, 1)

            pe.wait_ge(gI_done, 1)
            pe.matmul(ps[C:C1, 2, 0:C], ones[0:C, 0:1], gI[:, :], start=True, stop=True).then_inc(msum_done, 1)
            pe.wait_ge(mscale_done, 1)
            pe.matmul(ps[0:C, 3, 0:C], ones[C:C1, 0:C], rw[C:C1, 7, :], start=True, stop=True).then_inc(mb_done, 1)

            def fin(q, b, turn, first=False):
                pe.wait_ge(Sc_done, q + 1)
                pe.wait_ge(fin_in[b], 32 * turn + 32)
                if not first:
                    pe.wait_ge(f_y, q - 1)
                for k in range(4):
                    o = ps[:, 4 + b, k * C:(k + 1) * C]
                    pe.matmul(o, Sc[:, b, k * P:(k + 1) * P], Mm[:, :], start=True, stop=False)
                    last = pe.matmul(o, rE[:, b, k * P:(k + 1) * P], Mn[:, :], start=False, stop=True)
                last.then_inc(f_pe, 1)

            pe.wait_ge(M_done, 2)
            for b in range(2):
                fin(b, b, 0, True)
            with pe.Fori(1, QF // 2) as i:
                for b in range(2):
                    fin(2 * i + b, b, i)
            fin(QF, 0, QF // 2)

        @block.vector
        def _(dve):
            counts = {}

            def step(ins, done=chain):
                counts[done.name] = counts.get(done.name, 0) + 1
                ins.then_inc(done, 1)
                dve.wait_ge(done, counts[done.name])

            step(dve.memset(w12[C:C1, 0:C], 0.0), small_set)
            step(dve.memset(epsc[:, :], EPS), small_set)
            step(dve.memset(sink[:, :], SINK), small_set)
            dve.wait_ge(w_in, 16 * NW)
            step(dve.tensor_copy(basef[:, :], base[:, :]), basef_done)
            step(dve.memset(weS[:, :], 0.0), zeros_set)
            step(dve.memset(ones16, 1.0), zeros_set)
            step(dve.memset(zero8[:, :], 0.0), zeros_set)
            step(dve.tensor_copy(we16[:, 0, :], we[:, 0, :]), we_split)
            step(dve.tensor_tensor(we[:, 1, :], we[:, 0, :], we16[:, 0, :], ALU.subtract))
            step(dve.tensor_copy(we16[:, 1, :], we[:, 1, :]), we_split)
            step(dve.tensor_tensor(we[:, 2, :], we[:, 1, :], we16[:, 1, :], ALU.subtract))
            step(dve.tensor_copy(we16[:, 2, :], we[:, 2, :]), we_split)
            dve.wait_ge(dst_in, 16 * (1 + NDR))
            for k in range(NDR):
                n = min(P, NS - k * P)
                step(dve.tensor_copy(flag[0:n, 0:1], dst_r[k][0:n, 0:1]))
                step(dve.tensor_scalar(loc_r[k][0:n, :], dst_r[k][0:n, :], flag[0:n, 0:1], None, ALU.subtract),
                     loc_done)
            dve.wait_ge(baseb_done, 1)
            step(dve.tensor_tensor(dloc[:, :].rearrange("p (s t) -> p s t", t=TS),
                                   dst_t.rearrange("p (s t) -> p s t", t=TS),
                                   ps[:, 7, 0:NS].unsqueeze(2).to_broadcast([P, NS, TS]), ALU.subtract), dloc_done)
            step(dve.tensor_reduce(flag[:, 0:1], dloc[:, :], AX.X, ALU.max))
            step(dve.tensor_reduce(flag[:, 1:2], dloc[:, :], AX.X, ALU.min))
            step(dve.tensor_scalar(flag[:, 2:3], flag[:, 0:1], float(W), None, ALU.is_ge), badp_done)
            step(dve.tensor_scalar(flag[:, 3:4], flag[:, 1:2], 0.0, None, ALU.is_lt), badp_done)
            step(dve.memset(gacc[:, :], 0.0))
            step(dve.memset(eaS[:, :, :].rearrange("r b n -> r (b n)"), 0.0), ea_zero_set)

            for k in range(XP):
                b = k % 2
                dve.wait_ge(part_in[b], 16 * (k // 2 + 1))
                step(dve.tensor_copy(piece[b][0], part[b]))
                step(dve.tensor_tensor(part[b], part[b], piece[b][0], ALU.subtract))
                step(dve.tensor_copy(piece[b][1], part[b]))
                step(dve.tensor_tensor(part[b], part[b], piece[b][1], ALU.subtract))
                step(dve.tensor_copy(piece[b][2], part[b]), split_done)
            dve.wait_ge(bad_done, 1)
            step(dve.tensor_copy(flag[0:1, 0:2], ps[0:1, 6, 0:2]))
            step(dve.tensor_tensor(flag[0:1, 0:1], flag[0:1, 0:1], flag[0:1, 1:2], ALU.add))
            step(dve.tensor_copy(flagi[:, :], flag[0:1, 0:1]), flag_done)

            with dve.Fori(0, NPC // 2) as i:
                for b in range(2):
                    dve.wait_ge(st_relu, 2 * i + b + 1)
                    dve.scalar_tensor_tensor(out=Rst[b], in0=Rst[b], scalar=1.0, in1=Rst[b], op0=ALU.mult,
                                             op1=ALU.mult, accum_out=sumQ[:, bass.ds(2 * i + b, 1)]).then_inc(st_sq, 1)

            dve.wait_ge(st_sq, NPC)
            dve.wait_ge(nsq_done, NQS)
            for k, (src, count) in enumerate(((sumR, E), (nsR, N), (sumQ, E), (nsQ, N))):
                step(dve.tensor_reduce(col[:, k:k + 1], src[:, :], AX.X, ALU.add))
                step(dve.tensor_scalar(col[:, 4 + k:5 + k], col[:, k:k + 1], 1.0 / count, None, ALU.mult))
            mean, square = col[:, 4:6], col[:, 6:8]
            step(dve.tensor_tensor(col[:, 0:2], mean, mean, ALU.mult))
            step(dve.tensor_tensor(col[:, 2:4], square, col[:, 0:2], ALU.subtract), var_done)
            dve.wait_ge(sd_done, 1)
            step(dve.reciprocal(col[:, 8:10], col[:, 8:10]))
            step(dve.tensor_tensor(col[:, 10:12], col[:, 8:10], vec[:, 0:4:2], ALU.mult))
            step(dve.tensor_tensor(col[:, 0:2], col[:, 10:12], mean, ALU.mult))
            step(dve.tensor_tensor(col[:, 12:14], vec[:, 1:4:2], col[:, 0:2], ALU.subtract), shift_done)
            step(dve.tensor_scalar(w3p[0:C, :], w3[:, :], col[:, 10:11], None, ALU.mult), w3p_done)
            dve.wait_ge(consts, 4)
            step(dve.tensor_scalar(Mn[0:C, :], ident[0:C, 0:C], col[:, 11:12], None, ALU.mult))
            dve.wait_ge(const_done, 2)
            step(dve.tensor_copy(w3p[C:C1, :], ps[C:C1, 2, 0:C]), w3p_done)
            step(dve.tensor_copy(Mn[C:C1, :], ps[C:C1, 3, 0:C]), Mn_row_done)
            for b in range(2):
                dve.wait_ge(piece_out[b], 48 * XP)
            dve.wait_ge(ones_out, 128)
            step(dve.memset(S, 0.0))
            for b in range(2):
                dve.wait_ge(ab_out[b], 16 * NQS)
                dve.wait_ge(nR_out[b], 8 * NQS)
            step(dve.memset(rE[C:C1, :, :].rearrange("c b n -> c (b n)"), 1.0), ones_set)
            step(dve.memset(HXb[:, :, :, C:C1].rearrange("p b t o -> p (b t) o"), 1.0), ones_set)

            def oht(s, b, n):
                dve.wait_ge(dl_in[b], n * 16)
                dve.tensor_scalar(OHT[:, b, :], dlB[:, b, :], iota_p[0:KB, :], None, ALU.is_equal)\
                    .then_inc(oht_done, 1)

            def oh(s, b):
                dve.tensor_tensor(HXb[:, b, :, C1:HX], iota_w[:, :].unsqueeze(1).to_broadcast([P, TS, W]),
                                  dloc[:, bass.ds(s * TS, TS)].unsqueeze(2).to_broadcast([P, TS, W]), ALU.is_equal)\
                    .then_inc(oh_done, 1)

            def hpre(s, b, n, slot):
                dve.wait_ge(hmm_done, s + 1)
                dve.wait_ge(gathered[b], n * (16 * TS))
                dve.tensor_tensor(Hpre[:, b, :].rearrange("p (k n) -> p k n", k=2), ps[:, 2 + 2 * b:4 + 2 * b, 0:4 * C],
                                  G[:, slot, :].rearrange("p (k n) -> p k n", k=2), ALU.add).then_inc(hpre_done, 1)

            def sadd(s, b):
                first = dve.value_load(base[0:1, bass.ds(s, 1)], min_val=0, max_val=N)
                dve.wait_ge(scat_done, s + 1)
                win = S[:, bass.ds(first, W)]
                dve.tensor_tensor(win, win, ps[0:C1, 6 + b, C1:HX], ALU.add).then_inc(sadd_done, 1)
                dve.tensor_tensor(gacc[:, :], gacc[:, :], ps[0:C1, 6 + b, 0:C], ALU.add).then_inc(sadd_done, 1)

            dve.wait_ge(consts, 4)
            oht(0, 0, 1)
            oh(0, 0)
            oht(1, 1, 1)
            hpre(0, 0, 1, 0)
            oh(1, 1)
            dve.wait_ge(hmm_done, 1)
            oht(2, 0, 2)
            hpre(1, 1, 1, 1)
            dve.wait_ge(scat_done, 1)
            oh(2, 0)
            sadd(0, 0)
            dve.wait_ge(hmm_done, 2)
            oht(3, 1, 2)
            dve.wait_ge(hx_done, 1)
            hpre(2, 0, 2, 2)
            dve.wait_ge(scat_done, 2)
            oh(3, 1)
            with dve.Fori(1, (NS - 1) // 2 - 1) as i:
                for u in range(2):
                    s = 2 * i + u + 1
                    b = (u + 1) % 2
                    dve.wait_ge(sadd_done, 2 * s - 4)
                    sadd(s - 2, b)
                    dve.wait_ge(hmm_done, s)
                    oht(s + 1, 1 - b, i + 2)
                    dve.wait_ge(hx_done, s - 1)
                    hpre(s, b, i + (1 if u == 0 else 2), s % RS)
                    dve.wait_ge(scat_done, s)
                    oh(s + 1, 1 - b)
            for s in (NS - 2, NS - 1):
                b = s % 2
                dve.wait_ge(sadd_done, 2 * s - 4)
                sadd(s - 2, b)
                if s + 1 < NS:
                    dve.wait_ge(hmm_done, s)
                    oht(s + 1, 1 - b, (s + 1) // 2 + 1)
                dve.wait_ge(hx_done, s - 1)
                hpre(s, b, s // 2 + 1, s % RS)
                if s + 1 < NS:
                    dve.wait_ge(scat_done, s)
                    oh(s + 1, 1 - b)
            for s in (NS - 2, NS - 1):
                dve.wait_ge(sadd_done, 2 * s)
                sadd(s, s % 2)
            dve.wait_ge(sadd_done, 2 * NS)

            dve.wait_ge(flag_done, 1)
            with dve.If(dve.value_load(flagi[0:1, 0:1], min_val=0, max_val=2 * P) > 0):
                dve.wait_ge(gen_set, 1)
                dve.memset(gacc[:, :], 0.0).then_inc(gen_gacc, 1)
                dve.memset(S, 0.0).then_inc(gen_add, 1)
                dve.wait_ge(gen_gacc, 1)
                dve.wait_ge(gen_add, 1)
                dve.sem_inc(gen_free, 1)
                with dve.Fori(0, NT) as t:
                    dve.wait_ge(gen_in, 32 * t + 32)
                    dve.tensor_copy(dst_g, idx[:, 1:2]).then_inc(gen_dst, 1)
                    dve.wait_ge(gen_mm, t + 1)
                    dve.wait_ge(gen_rows, 32 * t + 32)
                    dve.tensor_tensor(Hpre[:, 0, 0:C], ps[:, 2, 0:C], g_rowA, ALU.add).then_inc(gen_half, 1)
                    dve.wait_ge(gen_half, t + 1)
                    dve.tensor_tensor(Hpre[:, 0, 0:C], Hpre[:, 0, 0:C], g_rowB, ALU.add).then_inc(gen_pre, 1)
                    dve.wait_ge(gen_gram, t + 1)
                    dve.tensor_tensor(gacc[:, :], gacc[:, :], ps[0:C1, 4, 0:C], ALU.add).then_inc(gen_gacc, 1)
                    dve.wait_ge(gen_gacc, t + 2)
                    dve.sem_inc(dve_turn, 1)
                    with dve.Fori(0, NG) as k:
                        dve.wait_ge(gen_dst, t * (NG + 1) + k + 1)
                        dve.tensor_scalar(oh_g, iota_g, dst_g, None, ALU.is_equal).then_inc(gen_oh, 1)
                        dve.wait_ge(gen_oh, t * NG + k + 1)
                        dve.tensor_scalar(dst_g, dst_g, -512.0, None, ALU.add).then_inc(gen_dst, 1)
                        dve.wait_ge(gen_sum, t * NG + k + 1)
                        chunk = S[:, bass.ds(k * 512, 512)]
                        dve.tensor_tensor(chunk, chunk, ps[0:C1, 3, :], ALU.add).then_inc(gen_add, 1)
                        dve.wait_ge(gen_add, t * NG + k + 2)
                    dve.sem_inc(gen_free, 1)

            step(dve.tensor_tensor(gI[:, :], gacc[0:C, :], ident[0:C, 0:C], ALU.mult), gI_done)
            at = slice(C, C1)
            step(dve.tensor_scalar(rw[at, 0, :], gacc[at, :], 1.0 / E, None, ALU.mult))
            step(dve.tensor_tensor(rw[at, 1, :], rw[at, 0, :], rw[at, 0, :], ALU.mult))
            dve.wait_ge(msum_done, 1)
            step(dve.tensor_scalar(rw[at, 2, :], ps[at, 2, 0:C], 1.0 / E, None, ALU.mult))
            step(dve.tensor_tensor(rw[at, 4, :], rw[at, 2, :], rw[at, 1, :], ALU.subtract), mvar_done)
            dve.wait_ge(msd_done, 1)
            step(dve.reciprocal(rw[at, 6, :], rw[at, 5, :]))
            step(dve.tensor_tensor(rw[at, 7, :], rw[at, 6, :], rows[at, 0, :], ALU.mult), mscale_done)
            step(dve.tensor_tensor(rw[at, 8, :], rw[at, 7, :], rw[at, 0, :], ALU.mult))
            step(dve.tensor_tensor(Mm[at, :], rows[at, 1, :], rw[at, 8, :], ALU.subtract), M_done)
            dve.wait_ge(mb_done, 1)
            step(dve.tensor_tensor(Mm[0:C, :], ident[0:C, 0:C], ps[0:C, 3, 0:C], ALU.mult), M_done)

            def fin_stats(q, b, turn, first=False):
                dve.wait_ge(f_pe, q + 1)
                dve.wait_ge(fin_in[b], 32 * turn + 32)
                dve.tensor_tensor(y[:, b, :], ps[:, 4 + b, 0:4 * C], xres[:, b, :], ALU.add).then_inc(f_y, 1)
                dve.wait_ge(f_y, q + 1)
                if not first:
                    dve.wait_ge(f_sd, q - 1)
                for k in range(4):
                    dve.bn_stats(bst[:, b, k, :], y[:, b, k * C:(k + 1) * C]).then_inc(f_bn, 1)
                dve.wait_ge(f_bn, 4 * q + 4)
                dve.sem_inc(dve_turn, 1)
                for k in range(4):
                    dve.bn_aggr(mv[:, b, k, :], bst[:, b, k, :]).then_inc(f_mv, 1)

            def fin_norm(q, b, turn):
                dve.wait_ge(f_sd, q + 1)
                dve.reciprocal(sd[:, b, 1, :], sd[:, b, 0, :]).then_inc(f_rs, 1)
                dve.wait_ge(f_rs, q + 1)
                if turn is not None:
                    dve.wait_ge(y_out[b], 16 * turn)
                for k in range(4):
                    dve.tensor_scalar(yo[:, b, k * C:(k + 1) * C], y[:, b, k * C:(k + 1) * C], mv[:, b, k, 0:1],
                                      sd[:, b, 1, k:k + 1], ALU.subtract, ALU.mult).then_inc(f_out, 1)

            fin_stats(0, 0, 0, True)
            fin_stats(1, 1, 0, True)
            fin_norm(0, 0, None)
            fin_stats(2, 0, 1)
            fin_norm(1, 1, None)
            with dve.Fori(1, QF // 2) as i:
                fin_stats(2 * i + 1, 1, i)
                fin_norm(2 * i, 0, i)
                fin_stats(2 * i + 2, 0, i + 1)
                fin_norm(2 * i + 1, 1, i)
            fin_norm(QF, 0, QF // 2)


def kernel(x, src, dst, edge_attr_4, **weights):
    import numpy as np
    import concourse.bacc as bacc
    from concourse import mybir as mb
    from concourse.bass_utils import run_bass_kernel_spmd

    x, src, dst, ea = (np.asarray(a) for a in (x, src, dst, edge_attr_4))
    N, C = x.shape
    E = src.shape[0]
    NS, NB = sizes(N, E)
    NP, NT = NB * P, NS * TS
    NTI = (NS // RS + 1) * RS * TS
    x_pad = np.zeros((NP, C), x.dtype)
    x_pad[:N] = x
    xT = np.zeros((C + 1, NP), x.dtype)
    xT[:C, :N] = x.T
    xT[C, :N] = 1
    src_pad = np.full((NTI * P,), NP, src.dtype)
    src_pad[:E] = src
    dst_pad = np.full((NT * P,), N, dst.dtype)
    dst_pad[:E] = dst
    eaT = np.zeros((ea.shape[1], (NS + 1) * SE), ea.dtype)
    eaT[:, :E] = ea.T
    arrays = {
        "x": x_pad, "xT": xT, "srcT": np.ascontiguousarray(src_pad.reshape(NTI, P).T),
        "dstT": np.ascontiguousarray(dst_pad.reshape(NT, P).T), "dst_rows": dst_pad.reshape(NS, SE), "eaT": eaT,
    }
    for name in ("W_node", "b_node", "g_node", "beta_node", "W_edge", "b_edge", "g_edge", "beta_edge",
                 "W_msg", "b_msg", "g_msg", "beta_msg"):
        arrays[name] = np.ascontiguousarray(weights["L0_gnn_" + name])

    nc = bacc.Bacc("TRN2", target_bir_lowering=False, num_devices=1)
    aps = {n: nc.dram_tensor(f"in_{n}", a.shape, mb.dt.from_np(a.dtype), kind="ExternalInput").ap()
           for n, a in arrays.items()}
    out = nc.dram_tensor("out", (N, C), F32, kind="ExternalOutput").ap()
    gnn_kernel(nc, out=out, E=E, **aps)
    r = run_bass_kernel_spmd(nc, [{f"in_{n}": a for n, a in arrays.items()}], core_ids=[0])
    return r.results[0]["out"]
```

```python
from contextlib import ExitStack

import concourse.bass as bass
from concourse import mybir

F32 = mybir.dt.float32
BF16 = mybir.dt.bfloat16
I32 = mybir.dt.int32
ALU = mybir.AluOpType
ACT = mybir.ActivationFunctionType
AX = mybir.AxisListType

P = 128
TS = 8
SE = TS * P
PC = 2 * SE
W = 64
KB = 96
KZ = 96
RS = 10
NQ = 512
EPS = 1e-5
SINK = -1.0e30


def sizes(N, E):
    NS = -(-E // SE)
    while NS % 100 != 3:
        NS += 1
    NB = -(-(N + KB) // P)
    return NS, NB + -NB % 4


def gnn_kernel(nc, x, xT, srcT, dstT, dst_rows, eaT, W_node, b_node, g_node, beta_node, W_edge, b_edge,
               g_edge, beta_edge, W_msg, b_msg, g_msg, beta_msg, out, E):
    N, C = out.shape
    C1 = C + 1
    NS, NB = sizes(N, E)
    NT = NS * TS
    NP = NB * P
    ED, EP = eaT.shape
    NPC = EP // PC
    XP = 8
    XC = ED * EP // P // XP
    SPLIT = XC + 3 * (XC // 2)
    NQS = NP // NQ
    NIT = (NS - 3) // 10
    NE = 2 * NIT
    HX = C1 + W
    assert C == 96 and ED == 4 and EP == (NS + 1) * SE and NPC % 2 == 0 and NE % RS == 0 and NS > NE + RS and RS > XP
    assert dst_rows.shape[0] == NS + 1 and N % 4 == 0 and (EP - E) % 2 == 0

    tabA = nc.dram_tensor("tabA", (NP + 1, C), F32).ap()
    tabB = nc.dram_tensor("tabB", (NP, C), F32).ap()
    nodeT = nc.dram_tensor("nodeT", (C, NP), F32).ap()
    stack = nc.dram_tensor("stack", (32, EP), BF16).ap()
    dloc_rows = nc.dram_tensor("dloc_rows", (NS + 1, SE), BF16).ap()
    spill = nc.dram_tensor("spill", (NE, P, TS * C), F32).ap()
    ea_flat = eaT.rearrange("r (k c) -> (r k) c", k=P // ED)
    stack_flat = [stack[4 * g:4 * g + 4, :].rearrange("r (k c) -> (r k) c", k=P // ED) for g in range(6)]

    with ExitStack() as ctx:
        def sb(name, shape, dt=F32):
            return ctx.enter_context(nc.sbuf_tensor(name, shape, dt))

        def sem(name):
            return ctx.enter_context(nc.semaphore(name))

        room = sb("room", [P, max(NP, 2 * SPLIT + EP // P // 2 + (EP - E) // 2)])
        S = room[0:C1, 0:NP]
        G = sb("G", [P, RS, TS * C])
        Gs = sb("Gs", [P, TS * C])
        NDR = -(-(NS + 1) // P)
        X2w = sb("X2", [P, max(NQS * 4 * C, NT + TS + NDR * SE * 3 // 2)])
        X2 = X2w[:, 0:NQS * 4 * C]
        rE = sb("rE", [C1, 2, SE])
        OHT = sb("OHT", [KB, 2, SE])
        HXb = sb("HXb", [P, 2, TS, HX])
        Hpre = sb("Hpre", [P, 2, TS * C])
        eaS = sb("eaS", [KZ, 2, PC], BF16)
        dlB = sb("dlB", [KB, 2, SE], BF16)
        Bw = sb("Bw", [KB, 2, C])
        dloc = sb("dloc", [P, NT + TS], BF16)
        idx_all = sb("idx_all", [P, srcT.shape[1]], I32)
        idx = sb("idx", [P, RS * TS], I32)
        base = sb("base", [1, NS + 1], I32)
        ident = sb("ident", [P, P])
        ones = sb("ones", [P, P])
        iota_w = sb("iota_w", [P, W], BF16)
        iota_p = sb("iota_p", [P, 1])
        w12 = sb("w12", [C1, 2 * C])
        w3 = sb("w3", [C, C])
        w3p = sb("w3p", [C1, C])
        wn = sb("wn", [C1, C])
        we = sb("we", [5, 3, C])
        we16 = sb("we16", [5, 3, C], BF16)
        weS = sb("weS", [KZ, C], BF16)
        vec = sb("vec", [C, 4])
        rows = sb("rows", [C1, 2, C])
        col = sb("col", [C, 16])
        rw = sb("rw", [C1, 9, C])
        sumR = sb("sumR", [C, NPC])
        sumQ = sb("sumQ", [C, NPC])
        nsR = sb("nsR", [C, NQS])
        nsQ = sb("nsQ", [C, NQS])
        gacc = sb("gacc", [C1, C])
        gI = sb("gI", [C, C])
        Mm = sb("Mm", [C1, C])
        Mn = sb("Mn", [C1, C])
        flag = sb("flag", [P, 4])
        flagi = sb("flagi", [1, 1], I32)
        sink = sb("sink", [1, C])
        bst = sb("bst", [P, 4, 4, 6])
        mv = sb("mv", [P, 4, 4, 2])
        sd = sb("sd", [P, 4, 2, 4])
        epsc = sb("epsc", [P, 1])
        ps = ctx.enter_context(nc.psum_tensor("ps", [P, 8, 512], F32))

        xc = HXb[:, :, :, :].rearrange("p b t n -> p (b t n)")[0:C1, 0:4 * NQ].rearrange("c (b n) -> c b n", b=4)
        Sc = HXb[0:C1, :, :, :].rearrange("c b t n -> c b (t n)")[:, :, 0:NQ]
        abS = Hpre[:, :, :].rearrange("p b n -> p (b n)").rearrange("p (b n) -> p b n", b=4)
        nR = rE[:, :, :].rearrange("c b n -> c (b n)").rearrange("c (b n) -> c b n", b=4)
        basef = rw[0:1, :, :].rearrange("o k c -> o (k c)")[:, 0:NS + 1]
        y = G[:, 0:4, 0:4 * C]
        yo = G[:, 4:8, 0:4 * C]

        g_rowA, g_rowB, iota_g, oh_g = G[:, 0, 0:C], G[:, 1, 0:C], G[:, 2, 0:512], G[:, 3, 0:512]
        dst_g, NG = flag[:, 0:1], NP // 512

        part = [room[:, b * SPLIT:b * SPLIT + XC] for b in range(2)]
        piece = [[room[:, b * SPLIT + XC + g * XC // 2:b * SPLIT + XC + (g + 1) * XC // 2].bitcast(BF16)
                  for g in range(3)] for b in range(2)]
        ones16 = room[:, 2 * SPLIT:2 * SPLIT + EP // P // 2].bitcast(BF16)
        zero8 = room[0:8, 2 * SPLIT + EP // P // 2:2 * SPLIT + EP // P // 2 + (EP - E) // 2].bitcast(BF16)
        NTD = NT + TS
        dst_t = X2w[:, 0:NTD].bitcast(I32)
        dst_r = [X2w[:, NTD + k * SE:NTD + (k + 1) * SE].bitcast(I32) for k in range(NDR)]
        loc_r = [X2w[:, NTD + NDR * SE + k * SE // 2:NTD + NDR * SE + (k + 1) * SE // 2].bitcast(BF16)
                 for k in range(NDR)]
        assert NS < 512
        Rst = [rE[0:C, :, :].rearrange("c b n -> c (b n)"), OHT[0:C, :, :].rearrange("c b n -> c (b n)")]

        w_in = sem("w_in")
        base_in = sem("base_in")
        wedge_in = sem("wedge_in")
        dst_in = sem("dst_in")
        idx_in = sem("idx_in")
        we_in = sem("we_in")
        wa_in = sem("wa_in")
        xc_in = [sem(f"xc_in{b}") for b in range(4)]
        a_out = [sem(f"a_out{b}") for b in range(4)]
        b_out = [sem(f"b_out{b}") for b in range(2)]
        x_in = sem("x_in")
        nR_in = [sem(f"nR_in{b}") for b in range(4)]
        spilled = [sem(f"spilled{b}") for b in range(2)]
        gs_in = sem("gs_in")
        nR_out = [sem(f"nR_out{b}") for b in range(2)]
        sink_out = sem("sink_out")
        part_in = [sem(f"part_in{b}") for b in range(2)]
        piece_out = [sem(f"piece_out{b}") for b in range(2)]
        ones_out = sem("ones_out")
        zero_out = sem("zero_out")
        loc_out = sem("loc_out")
        ea_in = [sem(f"ea_in{b}") for b in range(2)]
        dl_in = [sem(f"dl_in{b}") for b in range(2)]
        bw_in = [sem(f"bw_in{b}") for b in range(2)]
        gathered = [sem(f"gathered{b}") for b in range(2)]
        y_out = [sem(f"y_out{b}") for b in range(4)]
        consts = sem("consts")
        small_set = sem("small_set")
        zeros_set = sem("zeros_set")
        ea_zero_set = sem("ea_zero_set")
        ones_set = sem("ones_set")
        chain = sem("chain")
        ident_zero = sem("ident_zero")
        we_split = sem("we_split")
        basef_done = sem("basef_done")
        baseb_done = sem("baseb_done")
        dloc_done = sem("dloc_done")
        loc_done = sem("loc_done")
        badp_done = sem("badp_done")
        bad_done = sem("bad_done")
        flag_done = sem("flag_done")
        a_pe = sem("a_pe")
        a_copied = sem("a_copied")
        b_pe = sem("b_pe")
        b_act = sem("b_act")
        nvar_done = sem("nvar_done")
        nsd_done = sem("nsd_done")
        nshift_done = sem("nshift_done")
        Mn_done = sem("Mn_done")
        x2_pe = sem("x2_pe")
        x2_done = sem("x2_done")
        slot_free = sem("slot_free")
        nsq_done = sem("nsq_done")
        split_done = sem("split_done")
        st_pe = sem("st_pe")
        st_relu = sem("st_relu")
        st_sq = sem("st_sq")
        var_done = sem("var_done")
        sd_done = sem("sd_done")
        shift_done = sem("shift_done")
        const_done = sem("const_done")
        w3p_done = sem("w3p_done")
        idx_done = sem("idx_done")
        pool_turn = sem("pool_turn")
        dve_turn = sem("dve_turn")
        act_turn = sem("act_turn")
        z_done = sem("z_done")
        relz_done = sem("relz_done")
        oht_done = sem("oht_done")
        oh_done = sem("oh_done")
        hmm_done = sem("hmm_done")
        hpre_done = sem("hpre_done")
        hx_done = sem("hx_done")
        scat_done = sem("scat_done")
        sadd_done = sem("sadd_done")
        gen_set = sem("gen_set")
        gen_free = sem("gen_free")
        gen_in = sem("gen_in")
        gen_idx = sem("gen_idx")
        gen_rows = sem("gen_rows")
        gen_z = sem("gen_z")
        gen_relz = sem("gen_relz")
        gen_mm = sem("gen_mm")
        gen_dst = sem("gen_dst")
        gen_half = sem("gen_half")
        gen_pre = sem("gen_pre")
        gen_h = sem("gen_h")
        gen_gram = sem("gen_gram")
        gen_gacc = sem("gen_gacc")
        gen_oh = sem("gen_oh")
        gen_sum = sem("gen_sum")
        gen_add = sem("gen_add")
        gI_done = sem("gI_done")
        msum_done = sem("msum_done")
        mvar_done = sem("mvar_done")
        msd_done = sem("msd_done")
        mscale_done = sem("mscale_done")
        mb_done = sem("mb_done")
        M_done = sem("M_done")
        Sc_done = sem("Sc_done")
        f_pe = sem("f_pe")
        f_y = sem("f_y")
        f_bn = sem("f_bn")
        f_mv = sem("f_mv")
        f_sd = sem("f_sd")
        f_rs = sem("f_rs")
        f_out = sem("f_out")

        NW = 13
        HALF = RS // 2
        RINGS = NS // RS
        QF = N // 512
        REST = N - 512 * QF
        QT = QF // 4
        QB = QF + 1
        NPT = NPC // 2
        assert QF % 4 == 0 and REST and NP == 512 * QB

        def spilled_step(u):
            return u % 10 in (1, 6)

        def super_at(i, u):
            i, u = i + u // 10, u % 10
            return 2 * i + u // 6 if spilled_step(u) else NE + 3 + 8 * i + ring_step(u)

        def ring_step(u):
            return u - (u > 1) - (u > 6)

        def turn_at(i, u):
            return 5 * i + (3 + u) // 2 + 1

        block = ctx.enter_context(nc.Block())

        @block.sync
        def _(sp):
            sp.dma_start(w12[0:C, 0:C], W_msg[0:C, :]).then_inc(wa_in, 16)

            def load_xc(q, k):
                sp.dma_start(xc[:, k, :], xT[:, bass.ds(q * NQ, NQ)]).then_inc(xc_in[k], 16)

            for k in range(4):
                load_xc(k, k)
            with sp.Fori(0, QT - 1) as i:
                for k in range(4):
                    sp.wait_ge(a_pe, 4 * i + k + 1)
                    load_xc(4 * i + k + 4, k)
            sp.wait_ge(a_pe, QF - 3)
            load_xc(QF, 0)
            with nc.allow_non_contiguous_dma(reason="each super's first dst"):
                sp.dma_start(base[0:1, :], dst_rows[:, 0:1].rearrange("s o -> o s")).then_inc(base_in, 16)
            sp.dma_start(we[0:4, 0, :], W_edge).then_inc(wedge_in, 16)
            sp.dma_start(we[4:5, 0, :], b_edge[None, :]).then_inc(wedge_in, 16)
            sp.dma_start(dst_t, dstT).then_inc(dst_in, 16)
            for k in range(NDR):
                n = min(P, NS + 1 - k * P)
                sp.dma_start(dst_r[k][0:n, :], dst_rows[k * P:k * P + n, :]).then_inc(dst_in, 16)
            for b in range(2):
                sp.dma_start(part[b], ea_flat[:, b * XC:(b + 1) * XC]).then_inc(part_in[b], 16)
            sp.wait_ge(we_split, 3)
            sp.wait_ge(zeros_set, 3)
            for r, g in enumerate((0, 1, 2, 0, 1, 0)):
                sp.dma_start(weS[4 * r:4 * r + 4, :], we16[0:4, g, :]).then_inc(we_in, 16)
            for g in range(3):
                sp.dma_start(weS[24 + g:25 + g, :], we16[4:5, g, :]).then_inc(we_in, 16)
            sp.wait_ge(loc_done, NDR)
            for k in range(NDR):
                n = min(P, NS + 1 - k * P)
                sp.dma_start(dloc_rows[k * P:k * P + n, :], loc_r[k][0:n, :]).then_inc(loc_out, 16)

            def spill_out(s, slot, turn, first=False):
                b = slot % 2
                sp.wait_ge(gathered[b], turn * (16 * TS))
                sp.dma_start(spill[bass.ds(s, 1), :, :].rearrange("o p n -> (o p) n"), G[:, slot, :])\
                    .then_inc(spilled[b], 16)
                if not first:
                    sp.wait_ge(spilled[1 - b], (turn if b else turn - 1) * 16)
                    sp.sem_inc(slot_free, 1)

            for r in range(8):
                sp.dma_start(stack[24 + r:25 + r, :].rearrange("o (p c) -> (o p) c", p=P), ones16)\
                    .then_inc(ones_out, 16)
            for k in range(XP):
                b = k % 2
                sp.wait_ge(split_done, k + 1)
                for r, g in enumerate((0, 0, 0, 1, 1, 2)):
                    sp.dma_start(stack_flat[r][:, k * XC:(k + 1) * XC], piece[b][g]).then_inc(piece_out[b], 16)
                spill_out(k, k, k // 2 + 1, k == 0)
                if k + 2 < XP:
                    sp.wait_ge(piece_out[b], 96 * (k // 2 + 1))
                    sp.dma_start(part[b], ea_flat[:, (k + 2) * XC:(k + 3) * XC]).then_inc(part_in[b], 16)
            sp.wait_ge(ones_out, 128)
            sp.dma_start(stack[24:32, E:EP], zero8[:, :]).then_inc(zero_out, 16)
            for s in range(XP, RS):
                spill_out(s, s, s // 2 + 1)
            if NE > RS:
                with sp.Fori(1, NE // RS) as i:
                    for j in range(RS):
                        spill_out(i * RS + j, j, i * (RS // 2) + j // 2 + 1)
            sp.wait_ge(spilled[1], 16 * NE // 2)
            sp.sem_inc(slot_free, 1)

            def load_ea(s, b):
                sp.dma_start(eaS[0:32, b, 0:SE], stack[:, bass.ds(s * SE, SE)]).then_inc(ea_in[b], 16)

            def load_dl(s, b):
                sp.dma_start(dlB[:, b, :], dloc_rows[bass.ds(s, 1), :].to_broadcast([KB, SE]))\
                    .then_inc(dl_in[b], 16)

            def load_bw(s, b):
                first = sp.value_load(base[0:1, bass.ds(s, 1)], min_val=0, max_val=N)
                sp.dma_start(Bw[:, b, :], tabB[bass.ds(first, KB), :]).then_inc(bw_in[b], 16)

            def load_spilled(s):
                sp.dma_start(Gs[:, :], spill[bass.ds(s, 1), :, :].rearrange("o p n -> (o p) n")).then_inc(gs_in, 16)

            sp.wait_ge(st_pe, NPC)
            sp.wait_ge(st_sq, NPC)
            sp.wait_ge(loc_out, 16 * NDR)
            for b in range(2):
                sp.wait_ge(b_out[b], 16 * (QF // 2 + 1 - b))
            for n in range(3):
                if n == 2:
                    sp.wait_ge(z_done, 1)
                load_ea(NE + n, n % 2)
                if n == 2:
                    sp.wait_ge(oht_done, 1)
                load_dl(NE + n, n % 2)
                if n == 2:
                    sp.wait_ge(hmm_done, 1)
                load_bw(NE + n, n % 2)
            with sp.Fori(0, NIT) as i:
                for u in range(10):
                    n, b, s = 10 * i + 3 + u, (u + 1) % 2, super_at(i, u)
                    sp.wait_ge(z_done, n - 1)
                    load_ea(s, b)
                    sp.wait_ge(oht_done, n - 1)
                    load_dl(s, b)
                    sp.wait_ge(hmm_done, n - 1)
                    load_bw(s, b)
                    if spilled_step(u + 1):
                        sp.wait_ge(hpre_done, n - 2)
                        load_spilled(super_at(i, u + 1))
            sp.wait_ge(z_done, NS - 1)
            load_ea(NS, 1)
            sp.wait_ge(oht_done, NS - 1)
            load_dl(NS, 1)

            sp.wait_ge(flag_done, 1)
            with sp.If(sp.value_load(flagi[0:1, 0:1], min_val=0, max_val=2 * P) > 0):
                with sp.Fori(0, NT) as t:
                    sp.wait_ge(gen_free, t + 1)
                    sp.dma_start(eaS[0:32, 0, 0:P], stack[:, bass.ds(t * P, P)]).then_inc(gen_in, 16)
                    with nc.allow_non_contiguous_dma(reason="128 values of dst"):
                        sp.dma_start(idx[:, 1:2], dstT[:, bass.ds(t, 1)]).then_inc(gen_in, 16)
                sp.wait_ge(gen_free, NT + 1)

            def store_fin(q, k):
                sp.wait_ge(f_out, 4 * q + 4)
                sp.dma_start(out[bass.ds(q * NQ, NQ), :].rearrange("(p h) c -> p (h c)", h=4), yo[:, k, :])\
                    .then_inc(y_out[k], 16)

            with sp.Fori(0, QT) as i:
                for k in range(4):
                    store_fin(4 * i + k, k)
            sp.wait_ge(f_out, 4 * QF + 4)
            sp.dma_start(out[QF * NQ:N, :].rearrange("(p h) c -> p (h c)", h=4), yo[0:REST // 4, 0, :])\
                .then_inc(y_out[0], 16)
            for k in range(4):
                sp.wait_ge(y_out[k], 16 * (QT + (k == 0)))
            sp.wait_ge(ea_in[1], 16 * (NPT + turn_at(NIT, 0)))
            sp.wait_ge(dl_in[1], 16 * turn_at(NIT, 0))

        @block.gpsimd
        def _(pool):
            pool.memset(ones[:, :], 1.0).then_inc(consts, 1)
            pool.memset(ident[:, :], 0.0).then_inc(ident_zero, 1)
            pool.iota(iota_w[:, :], [[1, W]], base=0, channel_multiplier=0,
                      allow_small_or_imprecise_dtypes=True).then_inc(consts, 1)
            pool.iota(iota_p[:, :], [[0, 1]], base=0, channel_multiplier=1,
                      allow_small_or_imprecise_dtypes=True).then_inc(consts, 1)
            pool.wait_ge(ident_zero, 1)
            pool.affine_select(out=ident[:, :], in_=ident[:, :], compare_op=ALU.not_equal, fill=1.0, base=0,
                               pattern=[[-1, P]], channel_multiplier=1).then_inc(consts, 1)

            def copy_idx(col, half):
                pool.tensor_copy(idx[:, half * HALF * TS:(half + 1) * HALF * TS],
                                 idx_all[:, bass.ds(col, HALF * TS)]).then_inc(idx_done, 1)

            def gather(j):
                for t in range(TS):
                    pool.indirect_dma_start(G[:, j, t * C:(t + 1) * C], None, tabA,
                                            bass.IndirectOffsetOnAxis(ap=idx[:, j * TS + t:j * TS + t + 1], axis=0))\
                        .then_inc(gathered[j % 2], 16)

            pool.wait_ge(idx_in, 16)
            copy_idx(0, 0)
            copy_idx(HALF * TS, 1)
            for k in range(4):
                pool.wait_ge(a_out[k], 16 * (QT + (k == 0)))
            pool.wait_ge(sink_out, 16)
            pool.wait_ge(idx_done, 2)
            for j in range(RS):
                if j >= 2:
                    pool.wait_ge(gathered[j % 2], 16 * TS * (j // 2))
                gather(j)
                if j == HALF + 2:
                    copy_idx(RS * TS, 0)
            if RINGS > 1:
                with pool.Fori(1, RINGS) as it:
                    for j in range(RS):
                        s = it * RS + j
                        if j == 0:
                            pool.wait_ge(idx_done, 2 * it + 1)
                        if j == HALF:
                            pool.wait_ge(idx_done, 2 * it + 2)
                        pool.wait_ge(gathered[j % 2], (it * (RS // 2) + j // 2) * (16 * TS))
                        pool.wait_ge(slot_free, s - RS + 1)
                        pool.sem_inc(pool_turn, 1)
                        gather(j)
                        if j == 2:
                            copy_idx(it * (RS * TS) + HALF * TS, 1)
                        if j == HALF + 2:
                            copy_idx((it + 1) * (RS * TS), 0)
            for s in range(RINGS * RS, NS):
                j = s - RINGS * RS
                if j == 0:
                    pool.wait_ge(idx_done, 2 * RINGS + 1)
                if j == HALF:
                    pool.wait_ge(idx_done, 2 * RINGS + 2)
                pool.wait_ge(gathered[j % 2], 16 * TS * (s // 2))
                pool.wait_ge(slot_free, s - RS + 1)
                gather(j)
                if j == 2:
                    copy_idx(RINGS * RS * TS + HALF * TS, 1)

            pool.wait_ge(sadd_done, 2 * NS)
            pool.wait_ge(flag_done, 1)
            with pool.If(pool.value_load(flagi[0:1, 0:1], min_val=0, max_val=2 * P) > 0):
                pool.iota(iota_g, [[1, 512]], base=0, channel_multiplier=0,
                          allow_small_or_imprecise_dtypes=True).then_inc(gen_set, 1)
                with pool.Fori(0, NT) as t:
                    pool.wait_ge(gen_free, t + 1)
                    pool.sem_inc(pool_turn, 1)
                    pool.tensor_copy(idx[:, 0:1], idx_all[:, bass.ds(t, 1)]).then_inc(gen_idx, 1)
                    pool.wait_ge(gen_idx, t + 1)
                    pool.sem_inc(pool_turn, 1)
                    pool.wait_ge(gen_in, 32 * t + 32)
                    pool.sem_inc(pool_turn, 1)
                    pool.indirect_dma_start(g_rowA, None, tabA, bass.IndirectOffsetOnAxis(ap=idx[:, 0:1], axis=0))\
                        .then_inc(gen_rows, 16)
                    pool.indirect_dma_start(g_rowB, None, tabB, bass.IndirectOffsetOnAxis(ap=idx[:, 1:2], axis=0))\
                        .then_inc(gen_rows, 16)
                pool.wait_ge(gen_free, NT + 1)

            def fin_norm(q, k, turn):
                pool.wait_ge(f_rs, q + 1)
                pool.sem_inc(pool_turn, 1)
                if turn is not None:
                    pool.wait_ge(y_out[k], 16 * turn)
                    pool.sem_inc(pool_turn, 1)
                for h in range(4):
                    pool.tensor_scalar(yo[:, k, h * C:(h + 1) * C], y[:, k, h * C:(h + 1) * C], mv[:, k, h, 0:1],
                                       sd[:, k, 1, h:h + 1], ALU.subtract, ALU.mult).then_inc(f_out, 1)

            for k in range(4):
                fin_norm(k, k, None)
            with pool.Fori(1, QT) as i:
                for k in range(4):
                    fin_norm(4 * i + k, k, i)
            fin_norm(QF, 0, QT)

        @block.scalar
        def _(act):
            act.dma_start(idx_all[:, :], srcT).then_inc(idx_in, 16)
            act.wait_ge(small_set, 2)
            act.dma_start(tabA[NP:NP + 1, :], sink[:, :]).then_inc(sink_out, 16)

            def table_rows(tab, q):
                return tab[bass.ds(q * NQ, NQ), :].rearrange("(p h) c -> p (h c)", h=4)

            def a_step(q, k):
                act.wait_ge(a_copied, q + 1)
                act.dma_start(table_rows(tabA, q), abS[:, k, :]).then_inc(a_out[k], 16)

            with act.Fori(0, QT) as i:
                for k in range(4):
                    a_step(4 * i + k, k)
            a_step(QF, 0)

            act.wait_ge(a_pe, QB)
            for k in range(4):
                act.dma_start(xc[:, k, :], xT[:, k * NQ:(k + 1) * NQ]).then_inc(xc_in[k], 16)
            for dst, src in ((w12[0:C, C:2 * C], W_msg[C:2 * C, :]), (w12[C:C1, C:2 * C], b_msg[None, :]),
                             (wn[0:C, :], W_node), (wn[C:C1, :], b_node[None, :]),
                             (w3[:, :], W_msg[2 * C:3 * C, :]), (rows[C:C1, 0, :], g_msg[None, :]),
                             (rows[C:C1, 1, :], beta_msg[None, :])):
                act.dma_start(dst, src).then_inc(w_in, 16)
            with nc.allow_non_contiguous_dma(reason="four vectors as columns"):
                for k, v in enumerate((g_edge, beta_edge, g_node, beta_node)):
                    act.dma_start(vec[:, k:k + 1], v[:, None]).then_inc(w_in, 16)

            def b_step(q, k, turn, load):
                b = k % 2
                act.wait_ge(b_pe, q + 1)
                if load:
                    act.dma_start(xc[:, k, :], xT[:, bass.ds((q + 4) * NQ, NQ)]).then_inc(xc_in[k], 16)
                if turn is not None:
                    act.wait_ge(b_out[b], turn * 16)
                    act.wait_ge(nR_out[b], turn * 16)
                act.activation(abS[:, b, :], ps[:, b, 0:4 * C], ACT.Copy).then_inc(b_act, 1)
                act.activation(nR[0:C, b, :], ps[0:C, 2 + b, :], ACT.Relu, accum_out=nsR[:, bass.ds(q, 1)])\
                    .then_inc(b_act, 1)
                act.wait_ge(b_act, 2 * q + 2)
                act.dma_start(table_rows(tabB, q), abS[:, b, :]).then_inc(b_out[b], 16)
                act.dma_start(nodeT[:, bass.ds(q * NQ, NQ)], nR[0:C, b, :]).then_inc(nR_out[b], 16)
                act.activation(ps[0:C, 2 + b, :], nR[0:C, b, :], ACT.Square, accum_out=nsQ[:, bass.ds(q, 1)])\
                    .then_inc(nsq_done, 1)

            for k in range(4):
                act.wait_ge(a_out[k], 16 * (QT + (k == 0)))
            for k in range(4):
                b_step(k, k, k // 2 if k >= 2 else None, True)
            with act.Fori(1, QT - 1) as i:
                for k in range(4):
                    b_step(4 * i + k, k, 2 * i + k // 2, True)
            for k in range(4):
                b_step(QF - 4 + k, k, QF // 2 - 2 + k // 2, k == 0)
            b_step(QF, 0, QF // 2, False)

            act.wait_ge(dloc_done, 1)
            act.wait_ge(loc_out, 16 * NDR)
            act.dma_start(X2[:, :].rearrange("p (q n) -> p q n", q=QB), x.rearrange("(q p h) c -> p q (h c)", p=P, h=4))\
                .then_inc(x_in, 16)
            for b in range(2):
                act.wait_ge(nR_out[b], 16 * (QF // 2 + 1 - b))
            act.wait_ge(nsq_done, QB)

            def load_nR(q, k):
                act.dma_start(nR[0:C, k, :], nodeT[:, bass.ds(q * NQ, NQ)]).then_inc(nR_in[k], 16)

            for k in range(4):
                load_nR(k, k)
            act.wait_ge(nvar_done, 1)
            act.activation(col[:, 14:15], col[:, 13:14], ACT.Sqrt, bias=epsc[0:C, :]).then_inc(nsd_done, 1)
            with act.Fori(0, QT - 1) as i:
                for k in range(4):
                    act.wait_ge(x2_pe, 4 * i + k + 1)
                    load_nR(4 * i + k + 4, k)
            act.wait_ge(x2_pe, QF - 3)
            load_nR(QF, 0)

            def relu_step(c, b, waits, load=True):
                act.wait_ge(st_pe, c + 1)
                if load:
                    act.dma_start(eaS[0:32, b, :], stack[:, bass.ds((c + 2) * PC, PC)]).then_inc(ea_in[b], 16)
                if waits:
                    act.wait_ge(st_sq, c - 1)
                act.activation(Rst[b], ps[0:C, 4 * b:4 * b + 4, :].rearrange("c b n -> c (b n)"), ACT.Relu,
                               accum_out=sumR[:, bass.ds(c, 1)]).then_inc(st_relu, 1)

            for b in range(2):
                act.wait_ge(piece_out[b], 96 * XP // 2)
            act.wait_ge(zero_out, 16)
            act.wait_ge(ones_out, 128)
            act.wait_ge(ea_zero_set, 1)
            for c in range(2):
                act.dma_start(eaS[0:32, c, :], stack[:, c * PC:(c + 1) * PC]).then_inc(ea_in[c], 16)
            act.wait_ge(x2_pe, QB)
            for b in range(2):
                relu_step(b, b, False)
            with act.Fori(1, NPC // 2 - 1) as i:
                for b in range(2):
                    relu_step(2 * i + b, b, True)
            for b in range(2):
                relu_step(NPC - 2 + b, b, True, False)
            act.wait_ge(var_done, 1)
            act.activation(col[:, 6:7], col[:, 5:6], ACT.Sqrt, bias=epsc[0:C, :]).then_inc(sd_done, 1)

            def relz(s, b):
                act.wait_ge(z_done, s + 1)
                act.activation(rE[0:C, b, :], ps[0:C, 0:2, :].rearrange("c b n -> c (b n)"), ACT.Relu)\
                    .then_inc(relz_done, 1)

            def relh(s, b, ring=True):
                act.wait_ge(hpre_done, s + 1)
                if ring:
                    act.sem_inc(slot_free, 1)
                act.activation(HXb[:, b, :, 0:C], Hpre[:, b, :].rearrange("p (t c) -> p t c", t=TS), ACT.Relu)\
                    .then_inc(hx_done, 1)

            act.wait_ge(st_sq, NPC)
            relz(0, 0)
            relz(1, 1)
            relh(0, 0)
            act.wait_ge(hmm_done, 1)
            relz(2, 0)
            relh(1, 1)
            act.wait_ge(hmm_done, 2)
            relz(3, 1)
            act.wait_ge(scat_done, 1)
            relh(2, 0)
            with act.Fori(0, NIT) as i:
                for u in range(10):
                    n, b = 10 * i + 3 + u, (u + 1) % 2
                    act.wait_ge(hmm_done, n)
                    relz(n + 1, 1 - b)
                    act.wait_ge(scat_done, n - 1)
                    relh(n, b, not spilled_step(u))

            act.wait_ge(flag_done, 1)
            with act.If(act.value_load(flagi[0:1, 0:1], min_val=0, max_val=2 * P) > 0):
                with act.Fori(0, NT) as t:
                    act.wait_ge(gen_z, t + 1)
                    act.activation(rE[0:C, 0, 0:P], ps[0:C, 0, 0:P], ACT.Relu).then_inc(gen_relz, 1)
                    act.wait_ge(gen_pre, t + 1)
                    act.activation(HXb[:, 0, 0, 0:C], Hpre[:, 0, 0:C], ACT.Relu).then_inc(gen_h, 1)

            act.wait_ge(mvar_done, 1)
            act.activation(rw[C:C1, 5, :], rw[C:C1, 4, :], ACT.Sqrt, bias=epsc[C:C1, :]).then_inc(msd_done, 1)

            def fin_copy(q, b):
                act.activation(Sc[:, b, :], S[:, bass.ds(q * NQ, NQ)], ACT.Copy).then_inc(Sc_done, 1)

            def fin_sd(q, k, first):
                act.wait_ge(f_mv, 4 * q + 4)
                if not first:
                    act.wait_ge(f_out, 4 * q - 12)
                act.activation(sd[:, k, 0, :], mv[:, k, :, 1:2].rearrange("p h o -> p (h o)"), ACT.Sqrt,
                               bias=epsc[:, :]).then_inc(f_sd, 1)

            def fin_step(q, k, first=False, copy=True):
                act.wait_ge(f_pe, q + 1)
                act.sem_inc(act_turn, 1)
                if copy:
                    fin_copy(q + 2, k % 2)
                fin_sd(q, k, first)

            fin_copy(0, 0)
            fin_copy(1, 1)
            for k in range(4):
                fin_step(k, k, True)
            with act.Fori(1, QT - 1) as i:
                for k in range(4):
                    fin_step(4 * i + k, k)
            for k in range(4):
                fin_step(QF - 4 + k, k, copy=k < 3)
            fin_sd(QF, 0, False)

        @block.tensor
        def _(pe):
            def a_step(q, k, turn, first=False):
                pe.wait_ge(xc_in[k], turn * 16)
                if not first:
                    pe.wait_ge(a_copied, q - 3)
                for h in range(4):
                    last = pe.matmul(ps[:, k, h * C:(h + 1) * C], xc[0:C, k, h:NQ:4], w12[0:C, 0:C],
                                     start=True, stop=True)
                last.then_inc(a_pe, 1)

            pe.wait_ge(wa_in, 16)
            for k in range(4):
                a_step(k, k, 1, True)
            with pe.Fori(1, QT) as i:
                for k in range(4):
                    a_step(4 * i + k, k, i + 1)
            a_step(QF, 0, QT + 1)
            pe.wait_ge(consts, 4)
            pe.wait_ge(basef_done, 1)
            pe.matmul(ps[:, 7, 0:NS + 1], ones[0:1, :], basef, start=True, stop=True).then_inc(baseb_done, 1)

            def b_step(q, k, turn, first=False):
                b = k % 2
                pe.wait_ge(xc_in[k], turn * 16)
                if not first:
                    pe.wait_ge(nsq_done, q - 1)
                for h in range(4):
                    pe.matmul(ps[:, b, h * C:(h + 1) * C], xc[:, k, h:NQ:4], w12[:, C:2 * C], start=True, stop=True)
                pe.matmul(ps[0:C, 2 + b, :], wn[:, :], xc[:, k, :], start=True, stop=True).then_inc(b_pe, 1)

            pe.wait_ge(w_in, 16 * (NW - 2))
            pe.wait_ge(a_copied, QB)
            for k in range(4):
                b_step(k, k, QT + 1 + (k == 0), k < 2)
            with pe.Fori(1, QT) as i:
                for k in range(4):
                    b_step(4 * i + k, k, QT + 1 + (k == 0) + i)
            b_step(QF, 0, 2 * QT + 2)

            pe.wait_ge(nsq_done, QB)
            pe.wait_ge(nshift_done, 1)
            pe.matmul(ps[C:C1, 3, 0:C], col[:, 9:10], ident[0:C, 0:C], start=True, stop=True).then_inc(const_done, 1)

            def x2_step(q, k, turn, first=False):
                pe.wait_ge(nR_in[k], turn * 16)
                if not first:
                    pe.wait_ge(x2_done, q - 1)
                for h in range(4):
                    last = pe.matmul(ps[:, 4 + k % 2, h * C:(h + 1) * C], nR[:, k, h:NQ:4], Mn[:, :],
                                     start=True, stop=True)
                last.then_inc(x2_pe, 1)

            pe.wait_ge(Mn_done, 2)
            pe.wait_ge(ones_set, 1)
            for k in range(4):
                x2_step(k, k, 1, k < 2)
            with pe.Fori(1, QT) as i:
                for k in range(4):
                    x2_step(4 * i + k, k, i + 1)
            x2_step(QF, 0, QT + 1)
            pe.wait_ge(badp_done, 2)
            pe.matmul(ps[0:1, 6, 0:2], ones[:, 0:1], flag[:, 2:4], start=True, stop=True).then_inc(bad_done, 1)

            def stat_step(c, b, turn, first=False):
                pe.wait_ge(ea_in[b], turn * 16 + 16)
                if not first:
                    pe.wait_ge(st_relu, c - 1)
                for k in range(PC // 512):
                    last = pe.matmul(ps[0:C, 4 * b + k, :], weS[:, :], eaS[:, b, 512 * k:512 * k + 512],
                                     start=True, stop=True)
                last.then_inc(st_pe, 1)

            pe.wait_ge(we_in, 16 * 9)
            pe.wait_ge(ea_zero_set, 1)
            pe.wait_ge(x2_done, QB)
            pe.wait_ge(dloc_done, 1)
            pe.wait_ge(flag_done, 1)
            for b in range(2):
                stat_step(b, b, 0, True)
            with pe.Fori(1, NPC // 2) as i:
                for b in range(2):
                    stat_step(2 * i + b, b, i)
            pe.wait_ge(st_relu, NPC)
            pe.wait_ge(shift_done, 1)
            pe.matmul(ps[C:C1, 2, 0:C], col[:, 1:2], w3[:, :], start=True, stop=True).then_inc(const_done, 1)

            def zmm(s, b, n):
                pe.wait_ge(ea_in[b], n * 16)
                for k in range(2):
                    last = pe.matmul(ps[0:C, k, :], weS[:, :], eaS[:, b, 512 * k:512 * k + 512],
                                     start=True, stop=True)
                last.then_inc(z_done, 1)

            def hmm(s, b, n):
                pe.wait_ge(bw_in[b], n * 16)
                pe.wait_ge(oht_done, s + 1)
                for t in range(TS):
                    o = ps[:, 2 + 2 * b + t // 4, (t % 4) * C:(t % 4 + 1) * C]
                    pe.matmul(o, rE[:, b, t * P:(t + 1) * P], w3p[:, :], start=True, stop=False)
                    last = pe.matmul(o, OHT[:, b, t * P:(t + 1) * P], Bw[:, b, :], start=False, stop=True)
                last.then_inc(hmm_done, 1)

            def scat(s, b):
                pe.wait_ge(hx_done, s + 1)
                pe.wait_ge(oh_done, s + 1)
                for t in range(TS):
                    last = pe.matmul(ps[0:C1, 6 + b, 0:HX], HXb[:, b, t, 0:C1], HXb[:, b, t, :],
                                     start=(t == 0), stop=(t == TS - 1))
                last.then_inc(scat_done, 1)

            pe.wait_ge(w3p_done, 2)
            pe.wait_ge(ones_set, 2)
            zmm(0, 0, NPT + 1)
            pe.wait_ge(relz_done, 1)
            zmm(1, 1, NPT + 1)
            hmm(0, 0, 1)
            pe.wait_ge(relz_done, 2)
            zmm(2, 0, NPT + 2)
            hmm(1, 1, 1)
            scat(0, 0)
            pe.wait_ge(relz_done, 3)
            zmm(3, 1, NPT + 2)
            pe.wait_ge(hpre_done, 1)
            hmm(2, 0, 2)
            scat(1, 1)
            with pe.Fori(0, NIT) as i:
                for u in range(10):
                    n, b = 10 * i + 3 + u, (u + 1) % 2
                    pe.wait_ge(relz_done, n + 1)
                    zmm(n + 1, 1 - b, turn_at(i, u + 1) + NPT)
                    pe.wait_ge(hpre_done, n - 1)
                    hmm(n, b, turn_at(i, u))
                    pe.wait_ge(sadd_done, 2 * n - 4)
                    scat(n - 1, 1 - b)
            pe.wait_ge(sadd_done, 2 * NS - 4)
            scat(NS - 1, 0)

            pe.wait_ge(flag_done, 1)
            with pe.If(pe.value_load(flagi[0:1, 0:1], min_val=0, max_val=2 * P) > 0):
                with pe.Fori(0, NT) as t:
                    pe.wait_ge(gen_in, 32 * t + 32)
                    pe.matmul(ps[0:C, 0, 0:P], weS[:, :], eaS[:, 0, 0:P], start=True, stop=True).then_inc(gen_z, 1)
                    pe.wait_ge(gen_relz, t + 1)
                    pe.matmul(ps[:, 2, 0:C], rE[:, 0, 0:P], w3p[:, :], start=True, stop=True).then_inc(gen_mm, 1)
                    pe.wait_ge(gen_h, t + 1)
                    pe.matmul(ps[0:C1, 4, 0:C], HXb[:, 0, 0, 0:C1], HXb[:, 0, 0, 0:C],
                              start=True, stop=True).then_inc(gen_gram, 1)
                    with pe.Fori(0, NG) as k:
                        pe.wait_ge(gen_oh, t * NG + k + 1)
                        pe.matmul(ps[0:C1, 3, :], HXb[:, 0, 0, 0:C1], oh_g, start=True, stop=True)\
                            .then_inc(gen_sum, 1)

            pe.wait_ge(gI_done, 1)
            pe.matmul(ps[C:C1, 2, 0:C], ones[0:C, 0:1], gI[:, :], start=True, stop=True).then_inc(msum_done, 1)
            pe.wait_ge(mscale_done, 1)
            pe.matmul(ps[0:C, 3, 0:C], ones[C:C1, 0:C], rw[C:C1, 7, :], start=True, stop=True).then_inc(mb_done, 1)

            def fin(q, b, first=False):
                pe.wait_ge(Sc_done, q + 1)
                if not first:
                    pe.wait_ge(f_y, q - 1)
                for h in range(4):
                    last = pe.matmul(ps[:, 4 + b, h * C:(h + 1) * C], Sc[:, b, h:NQ:4], Mm[:, :],
                                     start=True, stop=True)
                last.then_inc(f_pe, 1)

            pe.wait_ge(M_done, 2)
            for b in range(2):
                fin(b, b, True)
            with pe.Fori(1, QF // 2) as i:
                for b in range(2):
                    fin(2 * i + b, b)
            fin(QF, 0)

        @block.vector
        def _(dve):
            counts = {}

            def step(ins, done=chain):
                counts[done.name] = counts.get(done.name, 0) + 1
                ins.then_inc(done, 1)
                dve.wait_ge(done, counts[done.name])

            step(dve.memset(epsc[:, :], EPS), small_set)
            step(dve.memset(sink[:, :], SINK), small_set)

            def a_step(q, k, turn):
                dve.wait_ge(a_pe, q + 1)
                if turn is not None:
                    dve.wait_ge(a_out[k], 16 * turn)
                dve.tensor_copy(abS[:, k, :], ps[:, k, 0:4 * C]).then_inc(a_copied, 1)

            for k in range(4):
                a_step(k, k, None)
            with dve.Fori(1, QT) as i:
                for k in range(4):
                    a_step(4 * i + k, k, i)
            a_step(QF, 0, QT)

            dve.wait_ge(base_in, 16)
            step(dve.tensor_copy(basef, base[:, :]), basef_done)
            step(dve.memset(weS[:, :], 0.0), zeros_set)
            step(dve.memset(ones16, 1.0), zeros_set)
            step(dve.memset(zero8, 0.0), zeros_set)
            dve.wait_ge(wedge_in, 32)
            step(dve.tensor_copy(we16[:, 0, :], we[:, 0, :]), we_split)
            step(dve.tensor_tensor(we[:, 1, :], we[:, 0, :], we16[:, 0, :], ALU.subtract))
            step(dve.tensor_copy(we16[:, 1, :], we[:, 1, :]), we_split)
            step(dve.tensor_tensor(we[:, 2, :], we[:, 1, :], we16[:, 1, :], ALU.subtract))
            step(dve.tensor_copy(we16[:, 2, :], we[:, 2, :]), we_split)
            dve.wait_ge(dst_in, 16 * (1 + NDR))
            for k in range(NDR):
                n = min(P, NS + 1 - k * P)
                step(dve.tensor_copy(flag[0:n, 0:1], dst_r[k][0:n, 0:1]))
                step(dve.tensor_scalar(loc_r[k][0:n, :], dst_r[k][0:n, :], flag[0:n, 0:1], None, ALU.subtract),
                     loc_done)
            dve.wait_ge(baseb_done, 1)
            step(dve.tensor_tensor(dloc[:, :].rearrange("p (s t) -> p s t", t=TS),
                                   dst_t.rearrange("p (s t) -> p s t", t=TS),
                                   ps[:, 7, 0:NS + 1].unsqueeze(2).to_broadcast([P, NS + 1, TS]), ALU.subtract),
                 dloc_done)
            step(dve.memset(gacc[:, :], 0.0))
            step(dve.memset(eaS[:, :, :].rearrange("r b n -> r (b n)"), 0.0), ea_zero_set)

            for k in range(XP):
                b = k % 2
                dve.wait_ge(part_in[b], 16 * (k // 2 + 1))
                step(dve.tensor_copy(piece[b][0], part[b]))
                step(dve.tensor_tensor(part[b], part[b], piece[b][0], ALU.subtract))
                step(dve.tensor_copy(piece[b][1], part[b]))
                step(dve.tensor_tensor(part[b], part[b], piece[b][1], ALU.subtract))
                step(dve.tensor_copy(piece[b][2], part[b]), split_done)
            step(dve.tensor_reduce(flag[:, 0:1], dloc[:, :], AX.X, ALU.max))
            step(dve.tensor_reduce(flag[:, 1:2], dloc[:, :], AX.X, ALU.min))
            step(dve.tensor_scalar(flag[:, 2:3], flag[:, 0:1], float(W), None, ALU.is_ge), badp_done)
            step(dve.tensor_scalar(flag[:, 3:4], flag[:, 1:2], 0.0, None, ALU.is_lt), badp_done)
            def norm_var(j, sums, squares, count, done):
                step(dve.tensor_reduce(col[:, j:j + 1], sums[:, :], AX.X, ALU.add))
                step(dve.tensor_reduce(col[:, j + 1:j + 2], squares[:, :], AX.X, ALU.add))
                step(dve.tensor_scalar(col[:, j + 2:j + 4], col[:, j:j + 2], 1.0 / count, None, ALU.mult))
                step(dve.tensor_tensor(col[:, j + 4:j + 5], col[:, j + 2:j + 3], col[:, j + 2:j + 3], ALU.mult))
                step(dve.tensor_tensor(col[:, j + 5:j + 6], col[:, j + 3:j + 4], col[:, j + 4:j + 5], ALU.subtract),
                     done)

            def norm_scale(j, gamma, beta, ready, done):
                dve.wait_ge(ready, 1)
                step(dve.reciprocal(col[:, j + 7:j + 8], col[:, j + 6:j + 7]))
                step(dve.tensor_tensor(col[:, j:j + 1], col[:, j + 7:j + 8], gamma, ALU.mult))
                step(dve.tensor_tensor(col[:, j + 4:j + 5], col[:, j:j + 1], col[:, j + 2:j + 3], ALU.mult))
                step(dve.tensor_tensor(col[:, j + 1:j + 2], beta, col[:, j + 4:j + 5], ALU.subtract), done)

            dve.wait_ge(w_in, 16 * (NW - 2))
            dve.wait_ge(nsq_done, QB)
            norm_var(8, nsR, nsQ, N, nvar_done)
            norm_scale(8, vec[:, 2:3], vec[:, 3:4], nsd_done, nshift_done)
            dve.wait_ge(consts, 4)
            step(dve.tensor_scalar(Mn[0:C, :], ident[0:C, 0:C], col[:, 8:9], None, ALU.mult), Mn_done)
            dve.wait_ge(const_done, 1)
            step(dve.tensor_copy(Mn[C:C1, :], ps[C:C1, 3, 0:C]), Mn_done)
            step(dve.memset(rE[C:C1, :, :].rearrange("c b n -> c (b n)"), 1.0), ones_set)
            dve.wait_ge(x_in, 16)

            def x2_step(q, b):
                dve.wait_ge(x2_pe, q + 1)
                rows_q = X2[:, bass.ds(q * (4 * C), 4 * C)]
                dve.tensor_tensor(rows_q, rows_q, ps[:, 4 + b, 0:4 * C], ALU.add).then_inc(x2_done, 1)

            with dve.Fori(0, QF // 2) as i:
                for b in range(2):
                    x2_step(2 * i + b, b)
            x2_step(QF, 0)

            dve.wait_ge(bad_done, 1)
            step(dve.tensor_copy(flag[0:1, 0:2], ps[0:1, 6, 0:2]))
            step(dve.tensor_tensor(flag[0:1, 0:1], flag[0:1, 0:1], flag[0:1, 1:2], ALU.add))
            step(dve.tensor_copy(flagi[:, :], flag[0:1, 0:1]), flag_done)

            for b in range(2):
                dve.wait_ge(piece_out[b], 48 * XP)
            dve.wait_ge(ones_out, 128)
            dve.wait_ge(zero_out, 16)
            dve.wait_ge(b_pe, QB)
            step(dve.memset(HXb[:, :, :, C:C1].rearrange("p b t o -> p (b t) o"), 1.0), ones_set)

            with dve.Fori(0, NPC // 2) as i:
                for b in range(2):
                    dve.wait_ge(st_relu, 2 * i + b + 1)
                    dve.scalar_tensor_tensor(out=Rst[b], in0=Rst[b], scalar=1.0, in1=Rst[b], op0=ALU.mult,
                                             op1=ALU.mult, accum_out=sumQ[:, bass.ds(2 * i + b, 1)]).then_inc(st_sq, 1)

            step(dve.memset(S, 0.0))
            dve.wait_ge(st_sq, NPC)
            norm_var(0, sumR, sumQ, E, var_done)
            norm_scale(0, vec[:, 0:1], vec[:, 1:2], sd_done, shift_done)
            step(dve.tensor_scalar(w3p[0:C, :], w3[:, :], col[:, 0:1], None, ALU.mult), w3p_done)
            dve.wait_ge(const_done, 2)
            step(dve.tensor_copy(w3p[C:C1, :], ps[C:C1, 2, 0:C]), w3p_done)

            def oht(s, b, n):
                dve.wait_ge(dl_in[b], n * 16)
                dve.tensor_scalar(OHT[:, b, :], dlB[:, b, :], iota_p[0:KB, :], None, ALU.is_equal)\
                    .then_inc(oht_done, 1)

            def oh(sup, b):
                dve.tensor_tensor(HXb[:, b, :, C1:HX], iota_w[:, :].unsqueeze(1).to_broadcast([P, TS, W]),
                                  dloc[:, bass.ds(sup * TS, TS)].unsqueeze(2).to_broadcast([P, TS, W]), ALU.is_equal)\
                    .then_inc(oh_done, 1)

            def hpre(n, b, sup):
                src = Gs[:, :] if sup is None else G[:, sup % RS, :]
                dve.wait_ge(hmm_done, n + 1)
                dve.tensor_tensor(Hpre[:, b, :].rearrange("p (k n) -> p k n", k=2), ps[:, 2 + 2 * b:4 + 2 * b, 0:4 * C],
                                  src.rearrange("p (k n) -> p k n", k=2), ALU.add).then_inc(hpre_done, 1)

            def sadd(n, b, sup):
                first = dve.value_load(base[0:1, bass.ds(sup, 1)], min_val=0, max_val=N)
                dve.wait_ge(scat_done, n + 1)
                win = S[:, bass.ds(first, W)]
                dve.tensor_tensor(win, win, ps[0:C1, 6 + b, C1:HX], ALU.add).then_inc(sadd_done, 1)
                dve.tensor_tensor(gacc[:, :], gacc[:, :], ps[0:C1, 6 + b, 0:C], ALU.add).then_inc(sadd_done, 1)

            oht(0, 0, 1)
            oh(NE, 0)
            oht(1, 1, 1)
            dve.wait_ge(gathered[0], (NE // 2 + 1) * (16 * TS))
            hpre(0, 0, NE)
            oh(NE + 1, 1)
            dve.wait_ge(hmm_done, 1)
            oht(2, 0, 2)
            dve.wait_ge(gathered[1], (NE // 2 + 1) * (16 * TS))
            hpre(1, 1, NE + 1)
            dve.wait_ge(scat_done, 1)
            oh(NE + 2, 0)
            sadd(0, 0, NE)
            dve.wait_ge(hmm_done, 2)
            oht(3, 1, 2)
            dve.wait_ge(hx_done, 1)
            dve.wait_ge(gathered[0], (NE // 2 + 2) * (16 * TS))
            hpre(2, 0, NE + 2)
            dve.wait_ge(scat_done, 2)
            oh(NE + 3, 1)
            with dve.Fori(0, NIT) as i:
                for u in range(10):
                    n, b = 10 * i + 3 + u, (u + 1) % 2
                    dve.wait_ge(sadd_done, 2 * n - 4)
                    sadd(n - 2, b, super_at(i, u - 2))
                    dve.wait_ge(hmm_done, n)
                    oht(n + 1, 1 - b, turn_at(i, u + 1))
                    dve.wait_ge(hx_done, n - 1)
                    if spilled_step(u):
                        dve.wait_ge(gs_in, 16 * (super_at(i, u) + 1))
                        hpre(n, b, None)
                    else:
                        r = 3 + ring_step(u)
                        dve.wait_ge(gathered[r % 2], (NE // 2 + 4 * i + r // 2 + 1) * (16 * TS))
                        hpre(n, b, super_at(i, u))
                    dve.wait_ge(scat_done, n)
                    oh(super_at(i, u + 1), 1 - b)
            for u in (8, 9):
                n = 10 * NIT - 7 + u
                dve.wait_ge(sadd_done, 2 * n)
                sadd(n, n % 2, super_at(NIT - 1, u))
            dve.wait_ge(sadd_done, 2 * NS)

            dve.wait_ge(flag_done, 1)
            with dve.If(dve.value_load(flagi[0:1, 0:1], min_val=0, max_val=2 * P) > 0):
                dve.wait_ge(gen_set, 1)
                dve.memset(gacc[:, :], 0.0).then_inc(gen_gacc, 1)
                dve.memset(S, 0.0).then_inc(gen_add, 1)
                dve.wait_ge(gen_gacc, 1)
                dve.wait_ge(gen_add, 1)
                dve.sem_inc(gen_free, 1)
                with dve.Fori(0, NT) as t:
                    dve.wait_ge(gen_in, 32 * t + 32)
                    dve.tensor_copy(dst_g, idx[:, 1:2]).then_inc(gen_dst, 1)
                    dve.wait_ge(gen_mm, t + 1)
                    dve.wait_ge(gen_rows, 32 * t + 32)
                    dve.tensor_tensor(Hpre[:, 0, 0:C], ps[:, 2, 0:C], g_rowA, ALU.add).then_inc(gen_half, 1)
                    dve.wait_ge(gen_half, t + 1)
                    dve.tensor_tensor(Hpre[:, 0, 0:C], Hpre[:, 0, 0:C], g_rowB, ALU.add).then_inc(gen_pre, 1)
                    dve.wait_ge(gen_gram, t + 1)
                    dve.tensor_tensor(gacc[:, :], gacc[:, :], ps[0:C1, 4, 0:C], ALU.add).then_inc(gen_gacc, 1)
                    dve.wait_ge(gen_gacc, t + 2)
                    dve.sem_inc(dve_turn, 1)
                    with dve.Fori(0, NG) as k:
                        dve.wait_ge(gen_dst, t * (NG + 1) + k + 1)
                        dve.tensor_scalar(oh_g, iota_g, dst_g, None, ALU.is_equal).then_inc(gen_oh, 1)
                        dve.wait_ge(gen_oh, t * NG + k + 1)
                        dve.tensor_scalar(dst_g, dst_g, -512.0, None, ALU.add).then_inc(gen_dst, 1)
                        dve.wait_ge(gen_sum, t * NG + k + 1)
                        chunk = S[:, bass.ds(k * 512, 512)]
                        dve.tensor_tensor(chunk, chunk, ps[0:C1, 3, :], ALU.add).then_inc(gen_add, 1)
                        dve.wait_ge(gen_add, t * NG + k + 2)
                    dve.sem_inc(gen_free, 1)

            step(dve.tensor_tensor(gI[:, :], gacc[0:C, :], ident[0:C, 0:C], ALU.mult), gI_done)
            at = slice(C, C1)
            step(dve.tensor_scalar(rw[at, 0, :], gacc[at, :], 1.0 / E, None, ALU.mult))
            step(dve.tensor_tensor(rw[at, 1, :], rw[at, 0, :], rw[at, 0, :], ALU.mult))
            dve.wait_ge(msum_done, 1)
            step(dve.tensor_scalar(rw[at, 2, :], ps[at, 2, 0:C], 1.0 / E, None, ALU.mult))
            step(dve.tensor_tensor(rw[at, 4, :], rw[at, 2, :], rw[at, 1, :], ALU.subtract), mvar_done)
            dve.wait_ge(msd_done, 1)
            step(dve.reciprocal(rw[at, 6, :], rw[at, 5, :]))
            step(dve.tensor_tensor(rw[at, 7, :], rw[at, 6, :], rows[at, 0, :], ALU.mult), mscale_done)
            step(dve.tensor_tensor(rw[at, 8, :], rw[at, 7, :], rw[at, 0, :], ALU.mult))
            step(dve.tensor_tensor(Mm[at, :], rows[at, 1, :], rw[at, 8, :], ALU.subtract), M_done)
            dve.wait_ge(mb_done, 1)
            step(dve.tensor_tensor(Mm[0:C, :], ident[0:C, 0:C], ps[0:C, 3, 0:C], ALU.mult), M_done)

            def fin_stats(q, k, turn):
                dve.wait_ge(f_pe, q + 1)
                if turn is not None:
                    dve.wait_ge(f_out, 4 * q - 12)
                dve.tensor_tensor(y[:, k, :], ps[:, 4 + k % 2, 0:4 * C], X2[:, bass.ds(q * (4 * C), 4 * C)], ALU.add)\
                    .then_inc(f_y, 1)
                dve.wait_ge(f_y, q + 1)
                for h in range(4):
                    dve.bn_stats(bst[:, k, h, :], y[:, k, h * C:(h + 1) * C]).then_inc(f_bn, 1)
                dve.wait_ge(f_bn, 4 * q + 4)
                dve.sem_inc(dve_turn, 1)
                for h in range(4):
                    dve.bn_aggr(mv[:, k, h, :], bst[:, k, h, :]).then_inc(f_mv, 1)

            def fin_rs(q, k):
                dve.wait_ge(f_sd, q + 1)
                dve.reciprocal(sd[:, k, 1, :], sd[:, k, 0, :]).then_inc(f_rs, 1)

            fin_stats(0, 0, None)
            for k in range(1, 4):
                fin_stats(k, k, None)
                fin_rs(k - 1, k - 1)
            with dve.Fori(1, QT) as i:
                for k in range(4):
                    fin_stats(4 * i + k, k, i)
                    fin_rs(4 * i + k - 1, (k - 1) % 4)
            fin_stats(QF, 0, QT)
            fin_rs(QF - 1, 3)
            fin_rs(QF, 0)


def kernel(x, src, dst, edge_attr_4, **weights):
    import numpy as np
    import concourse.bacc as bacc
    from concourse import mybir as mb
    from concourse.bass_utils import run_bass_kernel_spmd

    x, src, dst, ea = (np.asarray(a) for a in (x, src, dst, edge_attr_4))
    N, C = x.shape
    E = src.shape[0]
    NS, NB = sizes(N, E)
    NP, NT = NB * P, NS * TS
    NTI = (NS // RS + 1) * RS * TS
    x_pad = np.zeros((NP, C), x.dtype)
    x_pad[:N] = x
    xT = np.zeros((C + 1, NP), x.dtype)
    xT[:C, :N] = x.T
    xT[C, :N] = 1
    src_pad = np.full((NTI * P,), NP, src.dtype)
    src_pad[:E] = src
    dst_pad = np.full(((NT + TS) * P,), N, dst.dtype)
    dst_pad[:E] = dst
    eaT = np.zeros((ea.shape[1], (NS + 1) * SE), ea.dtype)
    eaT[:, :E] = ea.T
    arrays = {
        "x": x_pad, "xT": xT, "srcT": np.ascontiguousarray(src_pad.reshape(NTI, P).T),
        "dstT": np.ascontiguousarray(dst_pad.reshape(NT + TS, P).T), "dst_rows": dst_pad.reshape(NS + 1, SE), "eaT": eaT,
    }
    for name in ("W_node", "b_node", "g_node", "beta_node", "W_edge", "b_edge", "g_edge", "beta_edge",
                 "W_msg", "b_msg", "g_msg", "beta_msg"):
        arrays[name] = np.ascontiguousarray(weights["L0_gnn_" + name])

    nc = bacc.Bacc("TRN2", target_bir_lowering=False, num_devices=1)
    aps = {n: nc.dram_tensor(f"in_{n}", a.shape, mb.dt.from_np(a.dtype), kind="ExternalInput").ap()
           for n, a in arrays.items()}
    out = nc.dram_tensor("out", (N, C), F32, kind="ExternalOutput").ap()
    gnn_kernel(nc, out=out, E=E, **aps)
    r = run_bass_kernel_spmd(nc, [{f"in_{n}": a for n, a in arrays.items()}], core_ids=[0])
    return r.results[0]["out"]
```

```python
from contextlib import ExitStack

import concourse.bass as bass
from concourse import mybir

F32 = mybir.dt.float32
BF16 = mybir.dt.bfloat16
I32 = mybir.dt.int32
ALU = mybir.AluOpType
ACT = mybir.ActivationFunctionType
AX = mybir.AxisListType

P = 128
TS = 8
SE = TS * P
PC = 2 * SE
W = 64
KB = 96
KS = 36
KZ = 96
RS = 10
NQ = 512
EPS = 1e-5
SINK = -1.0e30


def sizes(N, E):
    NS = -(-E // SE)
    while NS % 100 != 3:
        NS += 1
    NB = -(-(N + W) // P)
    return NS, NB + -NB % 4


def gnn_kernel(nc, x, xT, srcT, dstT, dst_rows, eaT, W_node, b_node, g_node, beta_node, W_edge, b_edge,
               g_edge, beta_edge, W_msg, b_msg, g_msg, beta_msg, out, E):
    N, C = out.shape
    C1 = C + 1
    NS, NB = sizes(N, E)
    NT = NS * TS
    NP = NB * P
    ED, EP = eaT.shape
    NPC = -(-E // PC)
    LPC = E - (NPC - 1) * PC
    XP = 8
    XC = ED * EP // P // XP
    SPLIT = XC + 3 * (XC // 2)
    NQS = NP // NQ
    NIT = (NS - 3) // 10
    NE = 2 * NIT
    HX = C1 + W
    assert C == 96 and ED == 4 and EP == (NS + 1) * SE and NPC % 2 == 0 and NPC * PC <= EP and NE % RS == 0 and NS > NE + RS and RS > XP
    assert dst_rows.shape[0] == NS + 1 and N % 4 == 0

    tabA = nc.dram_tensor("tabA", (NP + 1, C), F32).ap()
    tabB = nc.dram_tensor("tabB", (NP, C), F32).ap()
    nodeT = nc.dram_tensor("nodeT", (C, NP), F32).ap()
    pieces = nc.dram_tensor("pieces", (3 * ED, EP), BF16).ap()
    dloc_rows = nc.dram_tensor("dloc_rows", (NS + 1, SE), BF16).ap()
    spill = nc.dram_tensor("spill", (NE, P, TS * C), F32).ap()
    ea_flat = eaT.rearrange("r (k c) -> (r k) c", k=P // ED)
    pieces_flat = [pieces[ED * g:ED * g + ED, :].rearrange("r (k c) -> (r k) c", k=P // ED) for g in range(3)]

    with ExitStack() as ctx:
        def sb(name, shape, dt=F32):
            return ctx.enter_context(nc.sbuf_tensor(name, shape, dt))

        def sem(name):
            return ctx.enter_context(nc.semaphore(name))

        room = sb("room", [P, max(NP, 2 * SPLIT)])
        S = room[0:C1, 0:NP]
        G = sb("G", [P, RS, TS * C])
        Gs = sb("Gs", [P, TS * C])
        NDR = -(-(NS + 1) // P)
        X2w = sb("X2", [P, max(NQS * 4 * C, NT + TS + NDR * SE * 3 // 2)])
        X2 = X2w[:, 0:NQS * 4 * C]
        rE = sb("rE", [C1, 2, SE])
        OHT = sb("OHT", [KB, 2, SE])
        HXb = sb("HXb", [P, 2, TS, HX])
        Hpre = sb("Hpre", [P, 2, TS * C])
        eaS = sb("eaS", [KZ, 2, PC], BF16)
        dlB = sb("dlB", [W, 2, SE], BF16)
        Bw = sb("Bw", [KB, 2, C])
        dloc = sb("dloc", [P, NT + TS], BF16)
        idx_all = sb("idx_all", [P, srcT.shape[1]], I32)
        idx = sb("idx", [P, RS * TS], I32)
        base = sb("base", [1, NS + 1], I32)
        ident = sb("ident", [P, P])
        ones = sb("ones", [P, P])
        iota_w = sb("iota_w", [P, W], BF16)
        iota_p = sb("iota_p", [P, 1])
        w12 = sb("w12", [C1, 2 * C])
        w3 = sb("w3", [C, C])
        w3p = sb("w3p", [C1, C])
        wn = sb("wn", [C1, C])
        we = sb("we", [ED, 3, C])
        we16 = sb("we16", [ED, 3, C], BF16)
        weS = sb("weS", [KZ, C], BF16)
        vec = sb("vec", [C, 4])
        be = sb("be", [C, 1])
        rows = sb("rows", [C1, 2, C])
        col = sb("col", [C, 16])
        rw = sb("rw", [C1, 9, C])
        sumR = sb("sumR", [C, NPC])
        sumQ = sb("sumQ", [C, NPC])
        nsR = sb("nsR", [C, NQS])
        nsQ = sb("nsQ", [C, NQS])
        gacc = sb("gacc", [C1, C])
        gI = sb("gI", [C, C])
        Mm = sb("Mm", [C1, C])
        Mn = sb("Mn", [C1, C])
        flag = sb("flag", [P, 4])
        flagi = sb("flagi", [1, 1], I32)
        sink = sb("sink", [1, C])
        bst = sb("bst", [P, 4, 4, 6])
        mv = sb("mv", [P, 4, 4, 2])
        sd = sb("sd", [P, 4, 3, 4])
        epsc = sb("epsc", [P, 1])
        ps = ctx.enter_context(nc.psum_tensor("ps", [P, 8, 512], F32))

        xc = HXb[:, :, :, :].rearrange("p b t n -> p (b t n)")[0:C1, 0:4 * NQ].rearrange("c (b n) -> c b n", b=4)
        Sc = HXb[0:C1, :, :, :].rearrange("c b t n -> c b (t n)")[:, :, 0:NQ]
        abS = Hpre[:, :, :].rearrange("p b n -> p (b n)").rearrange("p (b n) -> p b n", b=4)
        nR = rE[:, :, :].rearrange("c b n -> c (b n)").rearrange("c (b n) -> c b n", b=4)
        basef = rw[0:1, :, :].rearrange("o k c -> o (k c)")[:, 0:NS + 1]
        y = G[:, 0:4, 0:4 * C]
        yo = G[:, 4:8, 0:4 * C]

        g_rowA, g_rowB, iota_g, oh_g = G[:, 0, 0:C], G[:, 1, 0:C], G[:, 2, 0:512], G[:, 3, 0:512]
        dst_g, NG = flag[:, 0:1], NP // 512

        part = [room[:, b * SPLIT:b * SPLIT + XC] for b in range(2)]
        piece = [[room[:, b * SPLIT + XC + g * XC // 2:b * SPLIT + XC + (g + 1) * XC // 2].bitcast(BF16)
                  for g in range(3)] for b in range(2)]
        NTD = NT + TS
        dst_t = X2w[:, 0:NTD].bitcast(I32)
        dst_r = [X2w[:, NTD + k * SE:NTD + (k + 1) * SE].bitcast(I32) for k in range(NDR)]
        loc_r = [X2w[:, NTD + NDR * SE + k * SE // 2:NTD + NDR * SE + (k + 1) * SE // 2].bitcast(BF16)
                 for k in range(NDR)]
        assert NS < 512
        Rst = [rE[0:C, :, :].rearrange("c b n -> c (b n)"), OHT[0:C, :, :].rearrange("c b n -> c (b n)")]

        w_in = sem("w_in")
        base_in = sem("base_in")
        wedge_in = sem("wedge_in")
        dst_in = sem("dst_in")
        idx_in = sem("idx_in")
        we_in = sem("we_in")
        wa_in = sem("wa_in")
        xc_in = [sem(f"xc_in{b}") for b in range(4)]
        a_out = [sem(f"a_out{b}") for b in range(4)]
        b_out = [sem(f"b_out{b}") for b in range(2)]
        nR_in = [sem(f"nR_in{b}") for b in range(4)]
        spilled = [sem(f"spilled{b}") for b in range(2)]
        gs_in = sem("gs_in")
        nR_out = [sem(f"nR_out{b}") for b in range(2)]
        sink_out = sem("sink_out")
        part_in = [sem(f"part_in{b}") for b in range(2)]
        piece_out = [sem(f"piece_out{b}") for b in range(2)]
        loc_out = sem("loc_out")
        ea_in = [sem(f"ea_in{b}") for b in range(2)]
        dl_in = [sem(f"dl_in{b}") for b in range(2)]
        bw_in = [sem(f"bw_in{b}") for b in range(2)]
        gathered = [sem(f"gathered{b}") for b in range(2)]
        y_out = [sem(f"y_out{b}") for b in range(4)]
        consts = sem("consts")
        small_set = sem("small_set")
        zeros_set = sem("zeros_set")
        ea_zero_set = sem("ea_zero_set")
        w_zero_set = sem("w_zero_set")
        ones_set = sem("ones_set")
        chain = sem("chain")
        ident_zero = sem("ident_zero")
        we_split = sem("we_split")
        basef_done = sem("basef_done")
        baseb_done = sem("baseb_done")
        dloc_done = sem("dloc_done")
        loc_done = sem("loc_done")
        badp_done = sem("badp_done")
        bad_done = sem("bad_done")
        flag_done = sem("flag_done")
        a_pe = sem("a_pe")
        a_copied = sem("a_copied")
        b_pe = sem("b_pe")
        b_act = sem("b_act")
        nvar_done = sem("nvar_done")
        nsd_done = sem("nsd_done")
        nshift_done = sem("nshift_done")
        Mn_done = sem("Mn_done")
        x2_pe = sem("x2_pe")
        x2_done = sem("x2_done")
        slot_free = sem("slot_free")
        nsq_done = sem("nsq_done")
        split_done = sem("split_done")
        st_pe = sem("st_pe")
        st_relu = sem("st_relu")
        st_sq = sem("st_sq")
        var_done = sem("var_done")
        sd_done = sem("sd_done")
        shift_done = sem("shift_done")
        const_done = sem("const_done")
        w3p_done = sem("w3p_done")
        idx_done = sem("idx_done")
        pool_turn = sem("pool_turn")
        dve_turn = sem("dve_turn")
        act_turn = sem("act_turn")
        z_done = sem("z_done")
        relz_done = sem("relz_done")
        oht_done = sem("oht_done")
        oh_done = sem("oh_done")
        hmm_done = sem("hmm_done")
        hpre_done = sem("hpre_done")
        hx_done = sem("hx_done")
        scat_done = sem("scat_done")
        sadd_done = sem("sadd_done")
        gen_set = sem("gen_set")
        gen_free = sem("gen_free")
        gen_in = sem("gen_in")
        gen_idx = sem("gen_idx")
        gen_rows = sem("gen_rows")
        gen_z = sem("gen_z")
        gen_relz = sem("gen_relz")
        gen_mm = sem("gen_mm")
        gen_dst = sem("gen_dst")
        gen_half = sem("gen_half")
        gen_pre = sem("gen_pre")
        gen_h = sem("gen_h")
        gen_gram = sem("gen_gram")
        gen_gacc = sem("gen_gacc")
        gen_oh = sem("gen_oh")
        gen_sum = sem("gen_sum")
        gen_add = sem("gen_add")
        gI_done = sem("gI_done")
        msum_done = sem("msum_done")
        mvar_done = sem("mvar_done")
        msd_done = sem("msd_done")
        mscale_done = sem("mscale_done")
        mb_done = sem("mb_done")
        M_done = sem("M_done")
        Sc_done = sem("Sc_done")
        f_pe = sem("f_pe")
        f_y = sem("f_y")
        f_bn = sem("f_bn")
        f_mv = sem("f_mv")
        f_sd = sem("f_sd")
        f_rcp = sem("f_rcp")
        f_rs = sem("f_rs")
        f_out = sem("f_out")
        f_out_act = sem("f_out_act")

        NW = 12
        HALF = RS // 2
        RINGS = NS // RS
        QF = N // 512
        REST = N - 512 * QF
        QT = QF // 4
        QB = QF + 1
        NPT = NPC // 2
        assert QF % 4 == 0 and REST and NP == 512 * QB

        def spilled_step(u):
            return u % 10 in (1, 6)

        def super_at(i, u):
            i, u = i + u // 10, u % 10
            return 2 * i + u // 6 if spilled_step(u) else NE + 3 + 8 * i + ring_step(u)

        def ring_step(u):
            return u - (u > 1) - (u > 6)

        def turn_at(i, u):
            return 5 * i + (3 + u) // 2 + 1

        def attrs(first, n):
            return pieces[:, bass.ds(first, n)].unsqueeze(0).to_broadcast([3, 3 * ED, n])

        block = ctx.enter_context(nc.Block())

        @block.sync
        def _(sp):
            sp.dma_start(w12[0:C, 0:C], W_msg[0:C, :]).then_inc(wa_in, 16)

            def load_xc(q, k):
                sp.dma_start(xc[:, k, :], xT[:, bass.ds(q * NQ, NQ)]).then_inc(xc_in[k], 16)

            for k in range(4):
                load_xc(k, k)
            with sp.Fori(0, QT - 1) as i:
                for k in range(4):
                    sp.wait_ge(a_pe, 4 * i + k + 1)
                    load_xc(4 * i + k + 4, k)
            sp.wait_ge(a_pe, QF - 3)
            load_xc(QF, 0)
            with nc.allow_non_contiguous_dma(reason="each super's first dst"):
                sp.dma_start(base[0:1, :], dst_rows[:, 0:1].rearrange("s o -> o s")).then_inc(base_in, 16)
            sp.dma_start(we[0:4, 0, :], W_edge).then_inc(wedge_in, 16)
            sp.wait_ge(a_out[0], 16 * (QT + 1))
            sp.dma_start(dst_t, dstT).then_inc(dst_in, 16)
            for k in range(NDR):
                n = min(P, NS + 1 - k * P)
                sp.dma_start(dst_r[k][0:n, :], dst_rows[k * P:k * P + n, :]).then_inc(dst_in, 16)
            for b in range(2):
                sp.dma_start(part[b], ea_flat[:, b * XC:(b + 1) * XC]).then_inc(part_in[b], 16)
            sp.wait_ge(we_split, 3)
            sp.wait_ge(zeros_set, 1)
            for g in range(3):
                for r in range(3):
                    sp.dma_start(weS[12 * g + 4 * r:12 * g + 4 * r + 4, :], we16[:, g, :]).then_inc(we_in, 16)
            sp.wait_ge(loc_done, NDR)
            for k in range(NDR):
                n = min(P, NS + 1 - k * P)
                sp.dma_start(dloc_rows[k * P:k * P + n, :], loc_r[k][0:n, :]).then_inc(loc_out, 16)

            def spill_out(s, slot, turn, first=False):
                b = slot % 2
                sp.wait_ge(gathered[b], turn * (16 * TS))
                sp.dma_start(spill[bass.ds(s, 1), :, :].rearrange("o p n -> (o p) n"), G[:, slot, :])\
                    .then_inc(spilled[b], 16)
                if not first:
                    sp.wait_ge(spilled[1 - b], (turn if b else turn - 1) * 16)
                    sp.sem_inc(slot_free, 1)

            for k in range(XP):
                b = k % 2
                sp.wait_ge(split_done, k + 1)
                for g in range(3):
                    sp.dma_start(pieces_flat[g][:, k * XC:(k + 1) * XC], piece[b][g]).then_inc(piece_out[b], 16)
                spill_out(k, k, k // 2 + 1, k == 0)
                if k + 2 < XP:
                    sp.wait_ge(piece_out[b], 48 * (k // 2 + 1))
                    sp.dma_start(part[b], ea_flat[:, (k + 2) * XC:(k + 3) * XC]).then_inc(part_in[b], 16)
            for s in range(XP, RS):
                spill_out(s, s, s // 2 + 1)
            if NE > RS:
                with sp.Fori(1, NE // RS) as i:
                    for j in range(RS):
                        spill_out(i * RS + j, j, i * (RS // 2) + j // 2 + 1)
            sp.wait_ge(spilled[1], 16 * NE // 2)
            sp.sem_inc(slot_free, 1)

            def load_ea(s, b):
                sp.dma_start(eaS[0:KS, b, 0:SE], attrs(s * SE, SE)).then_inc(ea_in[b], 16)

            def load_dl(s, b):
                sp.dma_start(dlB[:, b, :], dloc_rows[bass.ds(s, 1), :].to_broadcast([W, SE]))\
                    .then_inc(dl_in[b], 16)

            def load_bw(s, b):
                first = sp.value_load(base[0:1, bass.ds(s, 1)], min_val=0, max_val=N)
                sp.dma_start(Bw[0:W, b, :], tabB[bass.ds(first, W), :]).then_inc(bw_in[b], 16)

            def load_spilled(s):
                sp.dma_start(Gs[:, :], spill[bass.ds(s, 1), :, :].rearrange("o p n -> (o p) n")).then_inc(gs_in, 16)

            sp.wait_ge(st_pe, NPC)
            sp.wait_ge(st_sq, NPC)
            sp.wait_ge(loc_out, 16 * NDR)
            for b in range(2):
                sp.wait_ge(b_out[b], 16 * (QF // 2 + 1 - b))
            for n in range(3):
                if n == 2:
                    sp.wait_ge(z_done, 1)
                load_ea(NE + n, n % 2)
                if n == 2:
                    sp.wait_ge(oht_done, 1)
                load_dl(NE + n, n % 2)
                if n == 2:
                    sp.wait_ge(hmm_done, 1)
                load_bw(NE + n, n % 2)
            with sp.Fori(0, NIT) as i:
                for u in range(10):
                    n, b, s = 10 * i + 3 + u, (u + 1) % 2, super_at(i, u)
                    sp.wait_ge(z_done, n - 1)
                    load_ea(s, b)
                    sp.wait_ge(oht_done, n - 1)
                    load_dl(s, b)
                    sp.wait_ge(hmm_done, n - 1)
                    load_bw(s, b)
                    if spilled_step(u + 1):
                        sp.wait_ge(hpre_done, n - 2)
                        load_spilled(super_at(i, u + 1))
            sp.wait_ge(z_done, NS - 1)
            load_ea(NS, 1)
            sp.wait_ge(oht_done, NS - 1)
            load_dl(NS, 1)

            sp.wait_ge(flag_done, 1)
            with sp.If(sp.value_load(flagi[0:1, 0:1], min_val=0, max_val=2 * P) > 0):
                with sp.Fori(0, NT) as t:
                    sp.wait_ge(gen_free, t + 1)
                    sp.dma_start(eaS[0:KS, 0, 0:P], attrs(t * P, P)).then_inc(gen_in, 16)
                    with nc.allow_non_contiguous_dma(reason="128 values of dst"):
                        sp.dma_start(idx[:, 1:2], dstT[:, bass.ds(t, 1)]).then_inc(gen_in, 16)
                sp.wait_ge(gen_free, NT + 1)

            def store_fin(q, k):
                sp.wait_ge(f_out, 2 * q + 2)
                sp.wait_ge(f_out_act, 2 * q + 2)
                sp.dma_start(out[bass.ds(q * NQ, NQ), :].rearrange("(p h) c -> p (h c)", h=4), yo[:, k, :])\
                    .then_inc(y_out[k], 16)

            with sp.Fori(0, QT) as i:
                for k in range(4):
                    store_fin(4 * i + k, k)
            sp.wait_ge(f_out, 2 * QF + 2)
            sp.wait_ge(f_out_act, 2 * QF + 2)
            sp.dma_start(out[QF * NQ:N, :].rearrange("(p h) c -> p (h c)", h=4), yo[0:REST // 4, 0, :])\
                .then_inc(y_out[0], 16)
            for k in range(4):
                sp.wait_ge(y_out[k], 16 * (QT + (k == 0)))
            sp.wait_ge(ea_in[1], 16 * (NPT + turn_at(NIT, 0)))
            sp.wait_ge(dl_in[1], 16 * turn_at(NIT, 0))

        @block.gpsimd
        def _(pool):
            pool.memset(ones[:, :], 1.0).then_inc(consts, 1)
            pool.memset(ident[:, :], 0.0).then_inc(ident_zero, 1)
            pool.iota(iota_w[:, :], [[1, W]], base=0, channel_multiplier=0,
                      allow_small_or_imprecise_dtypes=True).then_inc(consts, 1)
            pool.iota(iota_p[:, :], [[0, 1]], base=0, channel_multiplier=1,
                      allow_small_or_imprecise_dtypes=True).then_inc(consts, 1)
            pool.wait_ge(ident_zero, 1)
            pool.affine_select(out=ident[:, :], in_=ident[:, :], compare_op=ALU.not_equal, fill=1.0, base=0,
                               pattern=[[-1, P]], channel_multiplier=1).then_inc(consts, 1)

            def copy_idx(col, half):
                pool.tensor_copy(idx[:, half * HALF * TS:(half + 1) * HALF * TS],
                                 idx_all[:, bass.ds(col, HALF * TS)]).then_inc(idx_done, 1)

            def gather(j):
                for t in range(TS):
                    pool.indirect_dma_start(G[:, j, t * C:(t + 1) * C], None, tabA,
                                            bass.IndirectOffsetOnAxis(ap=idx[:, j * TS + t:j * TS + t + 1], axis=0))\
                        .then_inc(gathered[j % 2], 16)

            pool.wait_ge(idx_in, 16)
            copy_idx(0, 0)
            copy_idx(HALF * TS, 1)
            for k in range(4):
                pool.wait_ge(a_out[k], 16 * (QT + (k == 0)))
            pool.wait_ge(sink_out, 16)
            pool.wait_ge(idx_done, 2)
            for j in range(RS):
                if j >= 2:
                    pool.wait_ge(gathered[j % 2], 16 * TS * (j // 2))
                gather(j)
                if j == HALF + 2:
                    copy_idx(RS * TS, 0)
            if RINGS > 1:
                with pool.Fori(1, RINGS) as it:
                    for j in range(RS):
                        s = it * RS + j
                        if j == 0:
                            pool.wait_ge(idx_done, 2 * it + 1)
                        if j == HALF:
                            pool.wait_ge(idx_done, 2 * it + 2)
                        pool.wait_ge(gathered[j % 2], (it * (RS // 2) + j // 2) * (16 * TS))
                        pool.wait_ge(slot_free, s - RS + 1)
                        pool.sem_inc(pool_turn, 1)
                        gather(j)
                        if j == 2:
                            copy_idx(it * (RS * TS) + HALF * TS, 1)
                        if j == HALF + 2:
                            copy_idx((it + 1) * (RS * TS), 0)
            for s in range(RINGS * RS, NS):
                j = s - RINGS * RS
                if j == 0:
                    pool.wait_ge(idx_done, 2 * RINGS + 1)
                if j == HALF:
                    pool.wait_ge(idx_done, 2 * RINGS + 2)
                pool.wait_ge(gathered[j % 2], 16 * TS * (s // 2))
                pool.wait_ge(slot_free, s - RS + 1)
                gather(j)
                if j == 2:
                    copy_idx(RINGS * RS * TS + HALF * TS, 1)

            pool.wait_ge(sadd_done, 2 * NS)
            pool.wait_ge(flag_done, 1)
            with pool.If(pool.value_load(flagi[0:1, 0:1], min_val=0, max_val=2 * P) > 0):
                pool.iota(iota_g, [[1, 512]], base=0, channel_multiplier=0,
                          allow_small_or_imprecise_dtypes=True).then_inc(gen_set, 1)
                with pool.Fori(0, NT) as t:
                    pool.wait_ge(gen_free, t + 1)
                    pool.sem_inc(pool_turn, 1)
                    pool.tensor_copy(idx[:, 0:1], idx_all[:, bass.ds(t, 1)]).then_inc(gen_idx, 1)
                    pool.wait_ge(gen_idx, t + 1)
                    pool.sem_inc(pool_turn, 1)
                    pool.wait_ge(gen_in, 32 * t + 32)
                    pool.sem_inc(pool_turn, 1)
                    pool.indirect_dma_start(g_rowA, None, tabA, bass.IndirectOffsetOnAxis(ap=idx[:, 0:1], axis=0))\
                        .then_inc(gen_rows, 16)
                    pool.indirect_dma_start(g_rowB, None, tabB, bass.IndirectOffsetOnAxis(ap=idx[:, 1:2], axis=0))\
                        .then_inc(gen_rows, 16)
                pool.wait_ge(gen_free, NT + 1)

            def fin_norm(q, k, turn):
                pool.wait_ge(f_rs, q + 1)
                pool.sem_inc(pool_turn, 1)
                if turn is not None:
                    pool.wait_ge(y_out[k], 16 * turn)
                    pool.sem_inc(pool_turn, 1)
                for h in range(2):
                    pool.tensor_scalar(yo[:, k, h * C:(h + 1) * C], y[:, k, h * C:(h + 1) * C], mv[:, k, h, 0:1],
                                       sd[:, k, 1, h:h + 1], ALU.subtract, ALU.mult).then_inc(f_out, 1)

            for k in range(4):
                fin_norm(k, k, None)
            with pool.Fori(1, QT) as i:
                for k in range(4):
                    fin_norm(4 * i + k, k, i)
            fin_norm(QF, 0, QT)

        @block.scalar
        def _(act):
            act.wait_ge(small_set, 2)
            act.dma_start(tabA[NP:NP + 1, :], sink[:, :]).then_inc(sink_out, 16)

            def table_rows(tab, q):
                return tab[bass.ds(q * NQ, NQ), :].rearrange("(p h) c -> p (h c)", h=4)

            def a_step(q, k):
                act.wait_ge(a_copied, q + 1)
                act.dma_start(table_rows(tabA, q), abS[:, k, :]).then_inc(a_out[k], 16)

            for k in range(4):
                a_step(k, k)
            act.dma_start(idx_all[:, :], srcT).then_inc(idx_in, 16)
            with act.Fori(1, QT) as i:
                for k in range(4):
                    a_step(4 * i + k, k)
            a_step(QF, 0)

            act.wait_ge(a_pe, QB)
            for k in range(4):
                act.dma_start(xc[:, k, :], xT[:, k * NQ:(k + 1) * NQ]).then_inc(xc_in[k], 16)
            for dst, src in ((w12[0:C, C:2 * C], W_msg[C:2 * C, :]), (w12[C:C1, C:2 * C], b_msg[None, :]),
                             (wn[0:C, :], W_node), (wn[C:C1, :], b_node[None, :]),
                             (w3[:, :], W_msg[2 * C:3 * C, :]), (rows[C:C1, 0, :], g_msg[None, :]),
                             (rows[C:C1, 1, :], beta_msg[None, :])):
                act.dma_start(dst, src).then_inc(w_in, 16)
            with nc.allow_non_contiguous_dma(reason="vectors as columns"):
                for k, v in enumerate((g_edge, beta_edge, g_node, beta_node)):
                    act.dma_start(vec[:, k:k + 1], v[:, None]).then_inc(w_in, 16)
                act.dma_start(be[:, :], b_edge[:, None]).then_inc(w_in, 16)

            def b_step(q, k, turn, load):
                b = k % 2
                act.wait_ge(b_pe, q + 1)
                if load:
                    act.dma_start(xc[:, k, :], xT[:, bass.ds((q + 4) * NQ, NQ)]).then_inc(xc_in[k], 16)
                if turn is not None:
                    act.wait_ge(b_out[b], turn * 16)
                    act.wait_ge(nR_out[b], turn * 16)
                act.activation(abS[:, b, :], ps[:, b, 0:4 * C], ACT.Copy).then_inc(b_act, 1)
                act.activation(nR[0:C, b, :], ps[0:C, 2 + b, :], ACT.Relu, accum_out=nsR[:, bass.ds(q, 1)])\
                    .then_inc(b_act, 1)
                act.wait_ge(b_act, 2 * q + 2)
                act.dma_start(table_rows(tabB, q), abS[:, b, :]).then_inc(b_out[b], 16)
                act.dma_start(nodeT[:, bass.ds(q * NQ, NQ)], nR[0:C, b, :]).then_inc(nR_out[b], 16)
                act.activation(ps[0:C, 2 + b, :], nR[0:C, b, :], ACT.Square, accum_out=nsQ[:, bass.ds(q, 1)])\
                    .then_inc(nsq_done, 1)

            for k in range(4):
                act.wait_ge(a_out[k], 16 * (QT + (k == 0)))
            for k in range(4):
                b_step(k, k, k // 2 if k >= 2 else None, True)
            with act.Fori(1, QT - 1) as i:
                for k in range(4):
                    b_step(4 * i + k, k, 2 * i + k // 2, True)
            for k in range(4):
                b_step(QF - 4 + k, k, QF // 2 - 2 + k // 2, k == 0)
            b_step(QF, 0, QF // 2, False)

            act.wait_ge(dloc_done, 1)
            act.wait_ge(loc_out, 16 * NDR)
            for b in range(2):
                act.wait_ge(nR_out[b], 16 * (QF // 2 + 1 - b))
            act.wait_ge(nsq_done, QB)

            def load_nR(q, k):
                act.dma_start(nR[0:C, k, :], nodeT[:, bass.ds(q * NQ, NQ)]).then_inc(nR_in[k], 16)
                act.dma_start(X2[:, bass.ds(q * (4 * C), 4 * C)], table_rows(x, q)).then_inc(nR_in[k], 16)

            for k in range(4):
                load_nR(k, k)
            act.wait_ge(nvar_done, 1)
            act.activation(col[:, 14:15], col[:, 13:14], ACT.Sqrt, bias=epsc[0:C, :]).then_inc(nsd_done, 1)
            with act.Fori(0, QT - 1) as i:
                for k in range(4):
                    act.wait_ge(x2_pe, 4 * i + k + 1)
                    load_nR(4 * i + k + 4, k)
            act.wait_ge(x2_pe, QF - 3)
            load_nR(QF, 0)

            def relu_step(c, b, waits, load=True, n=PC):
                act.wait_ge(st_pe, c + 1)
                if load:
                    act.dma_start(eaS[0:KS, b, :], attrs((c + 2) * PC, PC)).then_inc(ea_in[b], 16)
                if waits:
                    act.wait_ge(st_sq, c - 1)
                act.activation(Rst[b][:, 0:n], ps[0:C, 4 * b:4 * b + 4, :].rearrange("c b n -> c (b n)")[:, 0:n],
                               ACT.Relu, bias=be[:, :], accum_out=sumR[:, bass.ds(c, 1)]).then_inc(st_relu, 1)

            act.wait_ge(w_in, 16 * NW)
            for b in range(2):
                act.wait_ge(piece_out[b], 48 * XP // 2)
            act.wait_ge(ea_zero_set, 1)
            for c in range(2):
                act.dma_start(eaS[0:KS, c, :], attrs(c * PC, PC)).then_inc(ea_in[c], 16)
            act.wait_ge(x2_pe, QB)
            for b in range(2):
                relu_step(b, b, False)
            with act.Fori(1, NPC // 2 - 1) as i:
                for b in range(2):
                    relu_step(2 * i + b, b, True)
            for b in range(2):
                relu_step(NPC - 2 + b, b, True, False, LPC if b else PC)
            act.wait_ge(var_done, 1)
            act.activation(col[:, 6:7], col[:, 5:6], ACT.Sqrt, bias=epsc[0:C, :]).then_inc(sd_done, 1)

            def relz(s, b):
                act.wait_ge(z_done, s + 1)
                act.activation(rE[0:C, b, :], ps[0:C, 0:2, :].rearrange("c b n -> c (b n)"), ACT.Relu, bias=be[:, :])\
                    .then_inc(relz_done, 1)

            def relh(s, b, ring=True):
                act.wait_ge(hpre_done, s + 1)
                if ring:
                    act.sem_inc(slot_free, 1)
                act.activation(HXb[:, b, :, 0:C], Hpre[:, b, :].rearrange("p (t c) -> p t c", t=TS), ACT.Relu)\
                    .then_inc(hx_done, 1)

            act.wait_ge(st_sq, NPC)
            relz(0, 0)
            relz(1, 1)
            relh(0, 0)
            act.wait_ge(hmm_done, 1)
            relz(2, 0)
            relh(1, 1)
            act.wait_ge(hmm_done, 2)
            relz(3, 1)
            act.wait_ge(scat_done, 1)
            relh(2, 0)
            with act.Fori(0, NIT) as i:
                for u in range(10):
                    n, b = 10 * i + 3 + u, (u + 1) % 2
                    act.wait_ge(hmm_done, n)
                    relz(n + 1, 1 - b)
                    act.wait_ge(scat_done, n - 1)
                    relh(n, b, not spilled_step(u))

            act.wait_ge(flag_done, 1)
            with act.If(act.value_load(flagi[0:1, 0:1], min_val=0, max_val=2 * P) > 0):
                with act.Fori(0, NT) as t:
                    act.wait_ge(gen_z, t + 1)
                    act.activation(rE[0:C, 0, 0:P], ps[0:C, 0, 0:P], ACT.Relu, bias=be[:, :])\
                        .then_inc(gen_relz, 1)
                    act.wait_ge(gen_pre, t + 1)
                    act.activation(HXb[:, 0, 0, 0:C], Hpre[:, 0, 0:C], ACT.Relu).then_inc(gen_h, 1)

            act.wait_ge(mvar_done, 1)
            act.activation(rw[C:C1, 5, :], rw[C:C1, 4, :], ACT.Sqrt, bias=epsc[C:C1, :]).then_inc(msd_done, 1)

            def fin_norm(q, k, turn):
                act.wait_ge(f_rs, q + 1)
                if turn is not None:
                    act.wait_ge(y_out[k], 16 * turn)
                for h in (2, 3):
                    act.activation(yo[:, k, h * C:(h + 1) * C], y[:, k, h * C:(h + 1) * C], ACT.Identity,
                                   bias=sd[:, k, 2, h:h + 1], scale=sd[:, k, 1, h:h + 1]).then_inc(f_out_act, 1)

            def fin_copy(q, b):
                act.activation(Sc[:, b, :], S[:, bass.ds(q * NQ, NQ)], ACT.Copy).then_inc(Sc_done, 1)

            def fin_sd(q, k, wait=True):
                act.wait_ge(f_mv, 4 * q + 4)
                if wait:
                    act.wait_ge(f_rs, q - 3)
                act.activation(sd[:, k, 0, :], mv[:, k, :, 1:2].rearrange("p h o -> p (h o)"), ACT.Sqrt,
                               bias=epsc[:, :]).then_inc(f_sd, 1)

            def fin_copy_next(q, k):
                act.wait_ge(f_pe, q + 1)
                act.sem_inc(act_turn, 1)
                fin_copy(q + 2, k % 2)

            fin_copy(0, 0)
            fin_copy(1, 1)
            for q in range(6):
                if q >= 1:
                    fin_sd(q - 1, (q - 1) % 4, q >= 5)
                fin_copy_next(q, q % 4)
                if q >= 2:
                    fin_norm(q - 2, (q - 2) % 4, None)
            with act.Fori(1, QT - 1) as i:
                for k in range(2, 6):
                    fin_sd(4 * i + k - 1, (k - 1) % 4)
                    fin_copy_next(4 * i + k, k % 4)
                    fin_norm(4 * i + k - 2, k - 2, i)
            for q in range(QF - 2, QF + 3):
                if q - 1 <= QF:
                    fin_sd(q - 1, (q - 1) % 4)
                if q + 2 <= QF:
                    fin_copy_next(q, q % 4)
                fin_norm(q - 2, (q - 2) % 4, (q - 2) // 4)

        @block.tensor
        def _(pe):
            def a_step(q, k, turn, first=False):
                pe.wait_ge(xc_in[k], turn * 16)
                if not first:
                    pe.wait_ge(a_copied, q - 3)
                for h in range(4):
                    last = pe.matmul(ps[:, k, h * C:(h + 1) * C], xc[0:C, k, h:NQ:4], w12[0:C, 0:C],
                                     start=True, stop=True)
                last.then_inc(a_pe, 1)

            pe.wait_ge(wa_in, 16)
            for k in range(4):
                a_step(k, k, 1, True)
            with pe.Fori(1, QT) as i:
                for k in range(4):
                    a_step(4 * i + k, k, i + 1)
            a_step(QF, 0, QT + 1)
            pe.wait_ge(consts, 4)
            pe.wait_ge(basef_done, 1)
            pe.matmul(ps[:, 7, 0:NS + 1], ones[0:1, :], basef, start=True, stop=True).then_inc(baseb_done, 1)

            def b_step(q, k, turn, first=False):
                b = k % 2
                pe.wait_ge(xc_in[k], turn * 16)
                if not first:
                    pe.wait_ge(nsq_done, q - 1)
                for h in range(4):
                    pe.matmul(ps[:, b, h * C:(h + 1) * C], xc[:, k, h:NQ:4], w12[:, C:2 * C], start=True, stop=True)
                pe.matmul(ps[0:C, 2 + b, :], wn[:, :], xc[:, k, :], start=True, stop=True).then_inc(b_pe, 1)

            pe.wait_ge(w_in, 16 * NW)
            pe.wait_ge(a_copied, QB)
            for k in range(4):
                b_step(k, k, QT + 1 + (k == 0), k < 2)
            with pe.Fori(1, QT) as i:
                for k in range(4):
                    b_step(4 * i + k, k, QT + 1 + (k == 0) + i)
            b_step(QF, 0, 2 * QT + 2)

            pe.wait_ge(nsq_done, QB)
            pe.wait_ge(nshift_done, 1)
            pe.matmul(ps[C:C1, 3, 0:C], col[:, 9:10], ident[0:C, 0:C], start=True, stop=True).then_inc(const_done, 1)

            def x2_step(q, k, turn, first=False):
                pe.wait_ge(nR_in[k], turn * 32)
                if not first:
                    pe.wait_ge(x2_done, q - 1)
                for h in range(4):
                    last = pe.matmul(ps[:, 4 + k % 2, h * C:(h + 1) * C], nR[:, k, h:NQ:4], Mn[:, :],
                                     start=True, stop=True)
                last.then_inc(x2_pe, 1)

            pe.wait_ge(Mn_done, 2)
            pe.wait_ge(ones_set, 1)
            for k in range(4):
                x2_step(k, k, 1, k < 2)
            with pe.Fori(1, QT) as i:
                for k in range(4):
                    x2_step(4 * i + k, k, i + 1)
            x2_step(QF, 0, QT + 1)
            pe.wait_ge(badp_done, 2)
            pe.matmul(ps[0:1, 6, 0:2], ones[:, 0:1], flag[:, 2:4], start=True, stop=True).then_inc(bad_done, 1)

            def stat_step(c, b, turn, first=False):
                pe.wait_ge(ea_in[b], turn * 16 + 16)
                if not first:
                    pe.wait_ge(st_relu, c - 1)
                for k in range(PC // 512):
                    last = pe.matmul(ps[0:C, 4 * b + k, :], weS[:, :], eaS[:, b, 512 * k:512 * k + 512],
                                     start=True, stop=True)
                last.then_inc(st_pe, 1)

            pe.wait_ge(we_in, 16 * 9)
            pe.wait_ge(ea_zero_set, 1)
            pe.wait_ge(x2_done, QB)
            pe.wait_ge(dloc_done, 1)
            pe.wait_ge(flag_done, 1)
            for b in range(2):
                stat_step(b, b, 0, True)
            with pe.Fori(1, NPC // 2) as i:
                for b in range(2):
                    stat_step(2 * i + b, b, i)
            pe.wait_ge(st_relu, NPC)
            pe.wait_ge(shift_done, 1)
            pe.matmul(ps[C:C1, 2, 0:C], col[:, 1:2], w3[:, :], start=True, stop=True).then_inc(const_done, 1)

            def zmm(s, b, n):
                pe.wait_ge(ea_in[b], n * 16)
                for k in range(2):
                    last = pe.matmul(ps[0:C, k, :], weS[:, :], eaS[:, b, 512 * k:512 * k + 512],
                                     start=True, stop=True)
                last.then_inc(z_done, 1)

            def hmm(s, b, n):
                pe.wait_ge(bw_in[b], n * 16)
                pe.wait_ge(oht_done, s + 1)
                for t in range(TS):
                    o = ps[:, 2 + 2 * b + t // 4, (t % 4) * C:(t % 4 + 1) * C]
                    pe.matmul(o, rE[:, b, t * P:(t + 1) * P], w3p[:, :], start=True, stop=False)
                    last = pe.matmul(o, OHT[:, b, t * P:(t + 1) * P], Bw[:, b, :], start=False, stop=True)
                last.then_inc(hmm_done, 1)

            def scat(s, b):
                pe.wait_ge(hx_done, s + 1)
                pe.wait_ge(oh_done, s + 1)
                for t in range(TS):
                    last = pe.matmul(ps[0:C1, 6 + b, 0:HX], HXb[:, b, t, 0:C1], HXb[:, b, t, :],
                                     start=(t == 0), stop=(t == TS - 1))
                last.then_inc(scat_done, 1)

            pe.wait_ge(w3p_done, 2)
            pe.wait_ge(ones_set, 2)
            pe.wait_ge(w_zero_set, 2)
            zmm(0, 0, NPT + 1)
            pe.wait_ge(relz_done, 1)
            zmm(1, 1, NPT + 1)
            hmm(0, 0, 1)
            pe.wait_ge(relz_done, 2)
            zmm(2, 0, NPT + 2)
            hmm(1, 1, 1)
            scat(0, 0)
            pe.wait_ge(relz_done, 3)
            zmm(3, 1, NPT + 2)
            pe.wait_ge(hpre_done, 1)
            hmm(2, 0, 2)
            scat(1, 1)
            with pe.Fori(0, NIT) as i:
                for u in range(10):
                    n, b = 10 * i + 3 + u, (u + 1) % 2
                    pe.wait_ge(relz_done, n + 1)
                    zmm(n + 1, 1 - b, turn_at(i, u + 1) + NPT)
                    pe.wait_ge(hpre_done, n - 1)
                    hmm(n, b, turn_at(i, u))
                    pe.wait_ge(sadd_done, 2 * n - 4)
                    scat(n - 1, 1 - b)
            pe.wait_ge(sadd_done, 2 * NS - 4)
            scat(NS - 1, 0)

            pe.wait_ge(flag_done, 1)
            with pe.If(pe.value_load(flagi[0:1, 0:1], min_val=0, max_val=2 * P) > 0):
                with pe.Fori(0, NT) as t:
                    pe.wait_ge(gen_in, 32 * t + 32)
                    pe.matmul(ps[0:C, 0, 0:P], weS[:, :], eaS[:, 0, 0:P], start=True, stop=True).then_inc(gen_z, 1)
                    pe.wait_ge(gen_relz, t + 1)
                    pe.matmul(ps[:, 2, 0:C], rE[:, 0, 0:P], w3p[:, :], start=True, stop=True).then_inc(gen_mm, 1)
                    pe.wait_ge(gen_h, t + 1)
                    pe.matmul(ps[0:C1, 4, 0:C], HXb[:, 0, 0, 0:C1], HXb[:, 0, 0, 0:C],
                              start=True, stop=True).then_inc(gen_gram, 1)
                    with pe.Fori(0, NG) as k:
                        pe.wait_ge(gen_oh, t * NG + k + 1)
                        pe.matmul(ps[0:C1, 3, :], HXb[:, 0, 0, 0:C1], oh_g, start=True, stop=True)\
                            .then_inc(gen_sum, 1)

            pe.wait_ge(gI_done, 1)
            pe.matmul(ps[C:C1, 2, 0:C], ones[0:C, 0:1], gI[:, :], start=True, stop=True).then_inc(msum_done, 1)
            pe.wait_ge(mscale_done, 1)
            pe.matmul(ps[0:C, 3, 0:C], ones[C:C1, 0:C], rw[C:C1, 7, :], start=True, stop=True).then_inc(mb_done, 1)

            def fin(q, b, first=False):
                pe.wait_ge(Sc_done, q + 1)
                if not first:
                    pe.wait_ge(f_y, q - 1)
                for h in range(4):
                    last = pe.matmul(ps[:, 4 + b, h * C:(h + 1) * C], Sc[:, b, h:NQ:4], Mm[:, :],
                                     start=True, stop=True)
                last.then_inc(f_pe, 1)

            pe.wait_ge(M_done, 2)
            for b in range(2):
                fin(b, b, True)
            with pe.Fori(1, QF // 2) as i:
                for b in range(2):
                    fin(2 * i + b, b)
            fin(QF, 0)

        @block.vector
        def _(dve):
            counts = {}

            def step(ins, done=chain):
                counts[done.name] = counts.get(done.name, 0) + 1
                ins.then_inc(done, 1)
                dve.wait_ge(done, counts[done.name])

            step(dve.memset(epsc[:, :], EPS), small_set)
            step(dve.memset(sink[:, :], SINK), small_set)

            def a_step(q, k, turn):
                dve.wait_ge(a_pe, q + 1)
                if turn is not None:
                    dve.wait_ge(a_out[k], 16 * turn)
                dve.tensor_copy(abS[:, k, :], ps[:, k, 0:4 * C]).then_inc(a_copied, 1)

            for k in range(4):
                a_step(k, k, None)
            with dve.Fori(1, QT) as i:
                for k in range(4):
                    a_step(4 * i + k, k, i)
            a_step(QF, 0, QT)

            dve.wait_ge(base_in, 16)
            step(dve.tensor_copy(basef, base[:, :]), basef_done)
            step(dve.memset(weS[:, :], 0.0), zeros_set)
            dve.wait_ge(wedge_in, 16)
            step(dve.tensor_copy(we16[:, 0, :], we[:, 0, :]), we_split)
            step(dve.tensor_tensor(we[:, 1, :], we[:, 0, :], we16[:, 0, :], ALU.subtract))
            step(dve.tensor_copy(we16[:, 1, :], we[:, 1, :]), we_split)
            step(dve.tensor_tensor(we[:, 2, :], we[:, 1, :], we16[:, 1, :], ALU.subtract))
            step(dve.tensor_copy(we16[:, 2, :], we[:, 2, :]), we_split)
            dve.wait_ge(dst_in, 16 * (1 + NDR))
            for k in range(NDR):
                n = min(P, NS + 1 - k * P)
                step(dve.tensor_copy(flag[0:n, 0:1], dst_r[k][0:n, 0:1]))
                step(dve.tensor_scalar(loc_r[k][0:n, :], dst_r[k][0:n, :], flag[0:n, 0:1], None, ALU.subtract),
                     loc_done)
            dve.wait_ge(baseb_done, 1)
            step(dve.tensor_tensor(dloc[:, :].rearrange("p (s t) -> p s t", t=TS),
                                   dst_t.rearrange("p (s t) -> p s t", t=TS),
                                   ps[:, 7, 0:NS + 1].unsqueeze(2).to_broadcast([P, NS + 1, TS]), ALU.subtract),
                 dloc_done)
            step(dve.memset(gacc[:, :], 0.0))
            step(dve.memset(eaS[:, :, :].rearrange("r b n -> r (b n)"), 0.0), ea_zero_set)

            for k in range(XP):
                b = k % 2
                dve.wait_ge(part_in[b], 16 * (k // 2 + 1))
                step(dve.tensor_copy(piece[b][0], part[b]))
                step(dve.tensor_tensor(part[b], part[b], piece[b][0], ALU.subtract))
                step(dve.tensor_copy(piece[b][1], part[b]))
                step(dve.tensor_tensor(part[b], part[b], piece[b][1], ALU.subtract))
                step(dve.tensor_copy(piece[b][2], part[b]), split_done)
            step(dve.tensor_reduce(flag[:, 0:1], dloc[:, :], AX.X, ALU.max))
            step(dve.tensor_reduce(flag[:, 1:2], dloc[:, :], AX.X, ALU.min))
            step(dve.tensor_scalar(flag[:, 2:3], flag[:, 0:1], float(W), None, ALU.is_ge), badp_done)
            step(dve.tensor_scalar(flag[:, 3:4], flag[:, 1:2], 0.0, None, ALU.is_lt), badp_done)
            def norm_var(j, sums, squares, count, done):
                step(dve.tensor_reduce(col[:, j:j + 1], sums[:, :], AX.X, ALU.add))
                step(dve.tensor_reduce(col[:, j + 1:j + 2], squares[:, :], AX.X, ALU.add))
                step(dve.tensor_scalar(col[:, j + 2:j + 4], col[:, j:j + 2], 1.0 / count, None, ALU.mult))
                step(dve.tensor_tensor(col[:, j + 4:j + 5], col[:, j + 2:j + 3], col[:, j + 2:j + 3], ALU.mult))
                step(dve.tensor_tensor(col[:, j + 5:j + 6], col[:, j + 3:j + 4], col[:, j + 4:j + 5], ALU.subtract),
                     done)

            def norm_scale(j, gamma, beta, ready, done):
                dve.wait_ge(ready, 1)
                step(dve.reciprocal(col[:, j + 7:j + 8], col[:, j + 6:j + 7]))
                step(dve.tensor_tensor(col[:, j:j + 1], col[:, j + 7:j + 8], gamma, ALU.mult))
                step(dve.tensor_tensor(col[:, j + 4:j + 5], col[:, j:j + 1], col[:, j + 2:j + 3], ALU.mult))
                step(dve.tensor_tensor(col[:, j + 1:j + 2], beta, col[:, j + 4:j + 5], ALU.subtract), done)

            dve.wait_ge(w_in, 16 * NW)
            dve.wait_ge(nsq_done, QB)
            norm_var(8, nsR, nsQ, N, nvar_done)
            norm_scale(8, vec[:, 2:3], vec[:, 3:4], nsd_done, nshift_done)
            dve.wait_ge(consts, 4)
            step(dve.tensor_scalar(Mn[0:C, :], ident[0:C, 0:C], col[:, 8:9], None, ALU.mult), Mn_done)
            dve.wait_ge(const_done, 1)
            step(dve.tensor_copy(Mn[C:C1, :], ps[C:C1, 3, 0:C]), Mn_done)
            step(dve.memset(rE[C:C1, :, :].rearrange("c b n -> c (b n)"), 1.0), ones_set)

            for b in range(2):
                dve.wait_ge(piece_out[b], 24 * XP)
            step(dve.memset(S, 0.0))
            dve.wait_ge(b_pe, QB)
            step(dve.memset(HXb[:, :, :, C:C1].rearrange("p b t o -> p (b t) o"), 1.0), ones_set)
            step(dve.memset(Bw[W:KB, :, :].rearrange("w b c -> w (b c)"), 0.0), w_zero_set)

            def x2_step(q, b):
                dve.wait_ge(x2_pe, q + 1)
                rows_q = X2[:, bass.ds(q * (4 * C), 4 * C)]
                dve.tensor_tensor(rows_q, rows_q, ps[:, 4 + b, 0:4 * C], ALU.add).then_inc(x2_done, 1)

            with dve.Fori(0, QF // 2) as i:
                for b in range(2):
                    x2_step(2 * i + b, b)
            x2_step(QF, 0)

            dve.wait_ge(bad_done, 1)
            step(dve.tensor_copy(flag[0:1, 0:2], ps[0:1, 6, 0:2]))
            step(dve.tensor_tensor(flag[0:1, 0:1], flag[0:1, 0:1], flag[0:1, 1:2], ALU.add))
            step(dve.tensor_copy(flagi[:, :], flag[0:1, 0:1]), flag_done)

            def square_step(c, b, n=PC):
                dve.wait_ge(st_relu, c + 1)
                dve.scalar_tensor_tensor(out=Rst[b][:, 0:n], in0=Rst[b][:, 0:n], scalar=1.0, in1=Rst[b][:, 0:n],
                                         op0=ALU.mult, op1=ALU.mult, accum_out=sumQ[:, bass.ds(c, 1)])\
                    .then_inc(st_sq, 1)

            with dve.Fori(0, NPC // 2 - 1) as i:
                for b in range(2):
                    square_step(2 * i + b, b)
            square_step(NPC - 2, 0)
            square_step(NPC - 1, 1, LPC)
            dve.wait_ge(st_sq, NPC)
            norm_var(0, sumR, sumQ, E, var_done)
            step(dve.memset(OHT[W:KB, :, :].rearrange("w b n -> w (b n)"), 0.0), w_zero_set)
            norm_scale(0, vec[:, 0:1], vec[:, 1:2], sd_done, shift_done)
            step(dve.tensor_scalar(w3p[0:C, :], w3[:, :], col[:, 0:1], None, ALU.mult), w3p_done)
            dve.wait_ge(const_done, 2)
            step(dve.tensor_copy(w3p[C:C1, :], ps[C:C1, 2, 0:C]), w3p_done)

            def oht(s, b, n):
                dve.wait_ge(dl_in[b], n * 16)
                dve.tensor_scalar(OHT[0:W, b, :], dlB[:, b, :], iota_p[0:W, :], None, ALU.is_equal)\
                    .then_inc(oht_done, 1)

            def oh(sup, b):
                dve.tensor_tensor(HXb[:, b, :, C1:HX], iota_w[:, :].unsqueeze(1).to_broadcast([P, TS, W]),
                                  dloc[:, bass.ds(sup * TS, TS)].unsqueeze(2).to_broadcast([P, TS, W]), ALU.is_equal)\
                    .then_inc(oh_done, 1)

            def hpre(n, b, sup):
                src = Gs[:, :] if sup is None else G[:, sup % RS, :]
                dve.wait_ge(hmm_done, n + 1)
                dve.tensor_tensor(Hpre[:, b, :].rearrange("p (k n) -> p k n", k=2), ps[:, 2 + 2 * b:4 + 2 * b, 0:4 * C],
                                  src.rearrange("p (k n) -> p k n", k=2), ALU.add).then_inc(hpre_done, 1)

            def sadd(n, b, sup):
                first = dve.value_load(base[0:1, bass.ds(sup, 1)], min_val=0, max_val=N)
                dve.wait_ge(scat_done, n + 1)
                win = S[:, bass.ds(first, W)]
                dve.tensor_tensor(win, win, ps[0:C1, 6 + b, C1:HX], ALU.add).then_inc(sadd_done, 1)
                dve.tensor_tensor(gacc[:, :], gacc[:, :], ps[0:C1, 6 + b, 0:C], ALU.add).then_inc(sadd_done, 1)

            oht(0, 0, 1)
            oh(NE, 0)
            oht(1, 1, 1)
            dve.wait_ge(gathered[0], (NE // 2 + 1) * (16 * TS))
            hpre(0, 0, NE)
            oh(NE + 1, 1)
            dve.wait_ge(hmm_done, 1)
            oht(2, 0, 2)
            dve.wait_ge(gathered[1], (NE // 2 + 1) * (16 * TS))
            hpre(1, 1, NE + 1)
            dve.wait_ge(scat_done, 1)
            oh(NE + 2, 0)
            sadd(0, 0, NE)
            dve.wait_ge(hmm_done, 2)
            oht(3, 1, 2)
            dve.wait_ge(hx_done, 1)
            dve.wait_ge(gathered[0], (NE // 2 + 2) * (16 * TS))
            hpre(2, 0, NE + 2)
            dve.wait_ge(scat_done, 2)
            oh(NE + 3, 1)
            with dve.Fori(0, NIT) as i:
                for u in range(10):
                    n, b = 10 * i + 3 + u, (u + 1) % 2
                    dve.wait_ge(sadd_done, 2 * n - 4)
                    sadd(n - 2, b, super_at(i, u - 2))
                    dve.wait_ge(hmm_done, n)
                    oht(n + 1, 1 - b, turn_at(i, u + 1))
                    dve.wait_ge(hx_done, n - 1)
                    if spilled_step(u):
                        dve.wait_ge(gs_in, 16 * (super_at(i, u) + 1))
                        hpre(n, b, None)
                    else:
                        r = 3 + ring_step(u)
                        dve.wait_ge(gathered[r % 2], (NE // 2 + 4 * i + r // 2 + 1) * (16 * TS))
                        hpre(n, b, super_at(i, u))
                    dve.wait_ge(scat_done, n)
                    oh(super_at(i, u + 1), 1 - b)
            for u in (8, 9):
                n = 10 * NIT - 7 + u
                dve.wait_ge(sadd_done, 2 * n)
                sadd(n, n % 2, super_at(NIT - 1, u))
            dve.wait_ge(sadd_done, 2 * NS)

            dve.wait_ge(flag_done, 1)
            with dve.If(dve.value_load(flagi[0:1, 0:1], min_val=0, max_val=2 * P) > 0):
                dve.wait_ge(gen_set, 1)
                dve.memset(gacc[:, :], 0.0).then_inc(gen_gacc, 1)
                dve.memset(S, 0.0).then_inc(gen_add, 1)
                dve.wait_ge(gen_gacc, 1)
                dve.wait_ge(gen_add, 1)
                dve.sem_inc(gen_free, 1)
                with dve.Fori(0, NT) as t:
                    dve.wait_ge(gen_in, 32 * t + 32)
                    dve.tensor_copy(dst_g, idx[:, 1:2]).then_inc(gen_dst, 1)
                    dve.wait_ge(gen_mm, t + 1)
                    dve.wait_ge(gen_rows, 32 * t + 32)
                    dve.tensor_tensor(Hpre[:, 0, 0:C], ps[:, 2, 0:C], g_rowA, ALU.add).then_inc(gen_half, 1)
                    dve.wait_ge(gen_half, t + 1)
                    dve.tensor_tensor(Hpre[:, 0, 0:C], Hpre[:, 0, 0:C], g_rowB, ALU.add).then_inc(gen_pre, 1)
                    dve.wait_ge(gen_gram, t + 1)
                    dve.tensor_tensor(gacc[:, :], gacc[:, :], ps[0:C1, 4, 0:C], ALU.add).then_inc(gen_gacc, 1)
                    dve.wait_ge(gen_gacc, t + 2)
                    dve.sem_inc(dve_turn, 1)
                    with dve.Fori(0, NG) as k:
                        dve.wait_ge(gen_dst, t * (NG + 1) + k + 1)
                        dve.tensor_scalar(oh_g, iota_g, dst_g, None, ALU.is_equal).then_inc(gen_oh, 1)
                        dve.wait_ge(gen_oh, t * NG + k + 1)
                        dve.tensor_scalar(dst_g, dst_g, -512.0, None, ALU.add).then_inc(gen_dst, 1)
                        dve.wait_ge(gen_sum, t * NG + k + 1)
                        chunk = S[:, bass.ds(k * 512, 512)]
                        dve.tensor_tensor(chunk, chunk, ps[0:C1, 3, :], ALU.add).then_inc(gen_add, 1)
                        dve.wait_ge(gen_add, t * NG + k + 2)
                    dve.sem_inc(gen_free, 1)

            step(dve.tensor_tensor(gI[:, :], gacc[0:C, :], ident[0:C, 0:C], ALU.mult), gI_done)
            at = slice(C, C1)
            step(dve.tensor_scalar(rw[at, 0, :], gacc[at, :], 1.0 / E, None, ALU.mult))
            step(dve.tensor_tensor(rw[at, 1, :], rw[at, 0, :], rw[at, 0, :], ALU.mult))
            dve.wait_ge(msum_done, 1)
            step(dve.tensor_scalar(rw[at, 2, :], ps[at, 2, 0:C], 1.0 / E, None, ALU.mult))
            step(dve.tensor_tensor(rw[at, 4, :], rw[at, 2, :], rw[at, 1, :], ALU.subtract), mvar_done)
            dve.wait_ge(msd_done, 1)
            step(dve.reciprocal(rw[at, 6, :], rw[at, 5, :]))
            step(dve.tensor_tensor(rw[at, 7, :], rw[at, 6, :], rows[at, 0, :], ALU.mult), mscale_done)
            step(dve.tensor_tensor(rw[at, 8, :], rw[at, 7, :], rw[at, 0, :], ALU.mult))
            step(dve.tensor_tensor(Mm[at, :], rows[at, 1, :], rw[at, 8, :], ALU.subtract), M_done)
            dve.wait_ge(mb_done, 1)
            step(dve.tensor_tensor(Mm[0:C, :], ident[0:C, 0:C], ps[0:C, 3, 0:C], ALU.mult), M_done)

            def fin_step(q, k, own=True, prev=True, prev2=True, wait=True):
                if own:
                    dve.wait_ge(f_pe, q + 1)
                    if wait:
                        dve.wait_ge(f_out, 2 * q - 6)
                        dve.wait_ge(f_out_act, 2 * q - 6)
                    dve.tensor_tensor(y[:, k, :], ps[:, 4 + k % 2, 0:4 * C], X2[:, bass.ds(q * (4 * C), 4 * C)],
                                      ALU.add).then_inc(f_y, 1)
                k1, k2 = (k - 1) % 4, (k - 2) % 4
                if prev2:
                    dve.wait_ge(f_sd, q - 1)
                    dve.reciprocal(sd[:, k2, 1, :], sd[:, k2, 0, :]).then_inc(f_rcp, 1)
                if prev:
                    dve.wait_ge(f_bn, 4 * q)
                    dve.sem_inc(dve_turn, 1)
                    for h in range(4):
                        dve.bn_aggr(mv[:, k1, h, :], bst[:, k1, h, :]).then_inc(f_mv, 1)
                if prev2:
                    dve.wait_ge(f_rcp, q - 1)
                    dve.scalar_tensor_tensor(out=sd[:, k2, 2, 2:4],
                                             in0=mv[:, k2, 2:4, 0:1].rearrange("p h o -> p (h o)"), scalar=-1.0,
                                             in1=sd[:, k2, 1, 2:4], op0=ALU.mult, op1=ALU.mult).then_inc(f_rs, 1)
                if own:
                    dve.wait_ge(f_y, q + 1)
                    for h in range(4):
                        dve.bn_stats(bst[:, k, h, :], y[:, k, h * C:(h + 1) * C]).then_inc(f_bn, 1)

            for q in range(4):
                fin_step(q, q, True, q >= 1, q >= 2, False)
            with dve.Fori(1, QT) as i:
                for k in range(4):
                    fin_step(4 * i + k, k)
            fin_step(QF, 0)
            fin_step(QF + 1, 1, own=False)
            fin_step(QF + 2, 2, own=False, prev=False)


def kernel(x, src, dst, edge_attr_4, **weights):
    import numpy as np
    import concourse.bacc as bacc
    from concourse import mybir as mb
    from concourse.bass_utils import run_bass_kernel_spmd

    x, src, dst, ea = (np.asarray(a) for a in (x, src, dst, edge_attr_4))
    N, C = x.shape
    E = src.shape[0]
    NS, NB = sizes(N, E)
    NP, NT = NB * P, NS * TS
    NTI = (NS // RS + 1) * RS * TS
    x_pad = np.zeros((NP, C), x.dtype)
    x_pad[:N] = x
    xT = np.zeros((C + 1, NP), x.dtype)
    xT[:C, :N] = x.T
    xT[C, :N] = 1
    src_pad = np.full((NTI * P,), NP, src.dtype)
    src_pad[:E] = src
    dst_pad = np.full(((NT + TS) * P,), N, dst.dtype)
    dst_pad[:E] = dst
    eaT = np.zeros((ea.shape[1], (NS + 1) * SE), ea.dtype)
    eaT[:, :E] = ea.T
    arrays = {
        "x": x_pad, "xT": xT, "srcT": np.ascontiguousarray(src_pad.reshape(NTI, P).T),
        "dstT": np.ascontiguousarray(dst_pad.reshape(NT + TS, P).T), "dst_rows": dst_pad.reshape(NS + 1, SE), "eaT": eaT,
    }
    for name in ("W_node", "b_node", "g_node", "beta_node", "W_edge", "b_edge", "g_edge", "beta_edge",
                 "W_msg", "b_msg", "g_msg", "beta_msg"):
        arrays[name] = np.ascontiguousarray(weights["L0_gnn_" + name])

    nc = bacc.Bacc("TRN2", target_bir_lowering=False, num_devices=1)
    aps = {n: nc.dram_tensor(f"in_{n}", a.shape, mb.dt.from_np(a.dtype), kind="ExternalInput").ap()
           for n, a in arrays.items()}
    out = nc.dram_tensor("out", (N, C), F32, kind="ExternalOutput").ap()
    gnn_kernel(nc, out=out, E=E, **aps)
    r = run_bass_kernel_spmd(nc, [{f"in_{n}": a for n, a in arrays.items()}], core_ids=[0])
    return r.results[0]["out"]
```
